# Optimizing a Trainium2 kernel written in Bass

```python
import numpy as np
import jax
import jax.numpy as jnp

def _softmax(x, axis=-1):
    return jax.nn.softmax(x, axis=axis)

def _gelu(x):
    return jax.nn.gelu(x, approximate=True)

def _silu(x):
    return jax.nn.silu(x)

def _sigmoid(x):
    return jax.nn.sigmoid(x)

def _layernorm(x, axis=-1, eps=1e-05):
    m = jnp.mean(x, axis=axis, keepdims=True)
    v = jnp.var(x, axis=axis, keepdims=True)
    return (x - m) / jnp.sqrt(v + eps)

def _scatter_add(tgt, idx, src, axis=0):
    return tgt.at[idx].add(src)

def _segment_sum(src, seg, n):
    return jax.ops.segment_sum(src, seg, n)
kernel_name = 'mk_gnn_preln_d2_gnn_r8_18647c'

def setup_inputs(seed: int=0):
    np.random.seed(seed)
    _w = jnp.asarray

    def _rec_inputs():
        import jax
        import jax.numpy as jnp
        _gk = jax.random.key(seed)
        x = -0.0005121 + 1.001 * jax.random.normal(jax.random.fold_in(_gk, 1), (6250, 64), jnp.float32)
        src = jax.random.randint(jax.random.fold_in(_gk, 2), (200000,), 0, 6250, jnp.int32)
        dst = jax.random.randint(jax.random.fold_in(_gk, 3), (200000,), 0, 6250, jnp.int32)
        _o = jnp.argsort(dst, stable=True)
        src = src[_o]
        dst = dst[_o]
        edge_type_16 = jax.random.randint(jax.random.fold_in(_gk, 12), (200000,), 0, 16, jnp.int32)
        edge_type_32 = jax.random.randint(jax.random.fold_in(_gk, 13), (200000,), 0, 32, jnp.int32)
        return (x, src, dst, edge_type_16, edge_type_32)
    x, src, dst, edge_type_16, edge_type_32 = _rec_inputs()

    def _L0_gnn_setup():
        import jax, jax.numpy as jnp
        import numpy as np
        N_NODES = 6250
        N_EDGES = 100000
        D_IN = 64
        D_OUT = 64
        NUM_RELS = 16
        key = jax.random.key(seed)
        k1, k2, k3, k4, k5 = jax.random.split(key, 5)
        feat = jax.random.normal(k1, (N_NODES, D_IN), dtype=jnp.float32)
        weight = jax.random.normal(k2, (NUM_RELS, D_IN, D_OUT), dtype=jnp.float32) * 0.05
        src = jax.random.randint(k3, (N_EDGES,), 0, N_NODES, dtype=jnp.int32)
        dst = jax.random.randint(k4, (N_EDGES,), 0, N_NODES, dtype=jnp.int32)
        etypes = jax.random.randint(k5, (N_EDGES,), 0, NUM_RELS, dtype=jnp.int32)
        return {'feat': feat, 'weight': weight, 'src': src, 'dst': dst, 'etypes': etypes}
    _L0_gnn_all = _L0_gnn_setup()
    _L0_gnn_in = {k: v for k, v in _L0_gnn_all.items() if k in ('weight',)}
    del _L0_gnn_all

    def _L1_gnn_setup():
        import jax, jax.numpy as jnp
        import numpy as np
        N_NODES = 12500
        N_EDGES = 125000
        IN_F = 64
        OUT_F = 64
        N_REL = 32
        N_BASES = 30
        key = jax.random.key(seed)
        k = jax.random.split(key, 8)
        node_features = jax.random.normal(k[0], (N_NODES, IN_F), dtype=jnp.float32)
        senders = jax.random.randint(k[1], (N_EDGES,), 0, N_NODES, dtype=jnp.int32)
        receivers = jax.random.randint(k[2], (N_EDGES,), 0, N_NODES, dtype=jnp.int32)
        relation_types = jax.random.randint(k[3], (N_EDGES,), 0, N_REL, dtype=jnp.int32)
        basis = jax.random.normal(k[4], (N_BASES, IN_F, OUT_F), dtype=jnp.float32) * 0.01
        coeff = jax.random.normal(k[5], (N_REL, N_BASES), dtype=jnp.float32) * 0.01
        self_weight = jax.random.normal(k[6], (IN_F, OUT_F), dtype=jnp.float32) * 0.01
        bias = jnp.zeros((OUT_F,), dtype=jnp.float32)
        return {'node_features': node_features, 'senders': senders, 'receivers': receivers, 'relation_types': relation_types, 'basis': basis, 'coeff': coeff, 'self_weight': self_weight, 'bias': bias}
    _L1_gnn_all = _L1_gnn_setup()
    _L1_gnn_in = {k: v for k, v in _L1_gnn_all.items() if k in ('basis', 'coeff', 'self_weight', 'bias')}
    del _L1_gnn_all
    return {'x': x, 'src': src, 'dst': dst, 'edge_type_16': edge_type_16, 'edge_type_32': edge_type_32, 'L0_gnn_weight': _L0_gnn_in['weight'], 'L1_gnn_basis': _L1_gnn_in['basis'], 'L1_gnn_coeff': _L1_gnn_in['coeff'], 'L1_gnn_self_weight': _L1_gnn_in['self_weight'], 'L1_gnn_bias': _L1_gnn_in['bias']}

def reference(x, src, dst, edge_type_16, edge_type_32, L0_gnn_weight, L1_gnn_basis, L1_gnn_coeff, L1_gnn_self_weight, L1_gnn_bias):
    import jax
    import jax.numpy as jnp

    def _L0_gnn_ref(feat, weight, src, dst, etypes):
        import jax, jax.numpy as jnp
        import numpy as np
        N_NODES = 6250
        N_EDGES = 100000
        D_IN = 64
        D_OUT = 64
        NUM_RELS = 16
        num_rels = weight.shape[0]
        h_src = feat[src]
        msg = jnp.zeros((h_src.shape[0], weight.shape[2]), dtype=feat.dtype)
        for r in range(num_rels):
            mask = etypes == r
            msg = msg + h_src * mask[:, None].astype(feat.dtype) @ weight[r]
        out = jax.ops.segment_sum(msg, dst, num_segments=feat.shape[0])
        return out

    def _L1_gnn_ref(node_features, senders, receivers, relation_types, basis, coeff, self_weight, bias):
        import jax, jax.numpy as jnp
        import numpy as np
        N_NODES = 12500
        N_EDGES = 125000
        IN_F = 64
        OUT_F = 64
        N_REL = 32
        N_BASES = 30
        num_nodes = node_features.shape[0]
        n_edges = senders.shape[0]
        rel_weights = jnp.einsum('rb,bio->rio', coeff, basis)
        src_features = node_features[senders]
        seg_ids = receivers * N_REL + relation_types
        agg = jax.ops.segment_sum(src_features, seg_ids, num_segments=num_nodes * N_REL)
        agg = agg.reshape(num_nodes, N_REL, node_features.shape[1])
        aggregated = jnp.einsum('nri,rio->no', agg, rel_weights)
        ones = jnp.ones((n_edges,), dtype=node_features.dtype)
        in_degree = jax.ops.segment_sum(ones, receivers, num_segments=num_nodes)
        in_degree = jnp.maximum(in_degree, 1.0)
        out = aggregated / in_degree[:, None]
        out = out + node_features @ self_weight
        out = out + bias
        return out
    h = jnp.maximum(_layernorm(x, axis=-1), 0.0)
    x = x + _L0_gnn_ref(h, L0_gnn_weight, src, dst, edge_type_16)
    h = jnp.maximum(_layernorm(x, axis=-1), 0.0)
    x = x + _L1_gnn_ref(h, src, dst, edge_type_32, L1_gnn_basis, L1_gnn_coeff, L1_gnn_self_weight, L1_gnn_bias)
    return x

_drawn_inputs = setup_inputs


def setup_inputs(seed=0):
    import zlib

    import numpy as np

    out = dict(_drawn_inputs(seed))
    spreads = {'L1_gnn_bias': (0.0, 0.1)}
    factors = {'L1_gnn_basis': 23.3, 'L1_gnn_coeff': 22.455}
    for name, (base, spread) in spreads.items():
        noise = np.random.default_rng([zlib.crc32(name.encode()), seed]).standard_normal(out[name].shape)
        drawn = base * np.exp(spread * noise) if base else spread * noise
        out[name] = jnp.asarray(drawn.astype(out[name].dtype))
    for name, factor in factors.items():
        out[name] = (out[name] * factor).astype(out[name].dtype)
    return out
```

```python
import concourse.bass as bass
from concourse import mybir
from contextlib import ExitStack


def two_layer_gnn_kernel(nc, x, src, dst, type16, type32, weight0, basis, coeff, self_weight, bias, out):
    f32, i32 = mybir.dt.float32, mybir.dt.int32
    ALU, ACT, AX = mybir.AluOpType, mybir.ActivationFunctionType, mybir.AxisListType

    N, D = x.shape
    E = src.shape[0]
    R = (weight0.shape[0], coeff.shape[0])
    NB = basis.shape[0]
    P = 128
    TT = 50
    NP = N // TT
    assert NP * TT == N and NP <= P
    CH = 10
    NCH = TT // CH
    CP = CH // 2
    STG = 5
    STEPS = [CP * R[l] * D // 512 for l in range(2)]
    UNITS = [STEPS[l] // 2 for l in range(2)]
    GT = 16
    GE = GT * P
    G = -(-E // GE)
    LASTE = E - (G - 1) * GE
    LASTT = -(-LASTE // P)
    WIN = P
    MAXW = (N - 1) // WIN + 1
    ROW = 80
    SPLIT = 112
    NO_NODE = -100000
    EPS = 1e-5

    table = [nc.dram_tensor(f"table{l}", (P * TT * R[l], D), f32, kind="Internal").ap() for l in range(2)]
    table_v = [table[l].rearrange("(p t r) f -> p t (r f)", p=P, t=TT) for l in range(2)]
    x_v = x.rearrange("(p t) f -> p (t f)", t=TT)
    out_v = out.rearrange("(p t) f -> p (t f)", t=TT)

    ctx = ExitStack()
    with ctx:
        def sb(name, shape, dt=f32):
            return ctx.enter_context(nc.sbuf_tensor(name, shape, dt))

        def sem(name):
            return ctx.enter_context(nc.semaphore(name))

        xs = sb("xs", [P, TT, D])
        h = sb("h", [P, CH, D])
        hT = sb("hT", [P, CP, P])
        accC = sb("accC", [D + 1, CH, P])
        accT = sb("accT", [D + 1, P * TT])
        W = [sb("W0", [P, R[0] * D]), sb("W1", [P, R[1] * D])]
        selfW = sb("selfW", [P, D])
        biasB = sb("biasB", [P, D])
        keyT = [sb("keyT0", [P, G, GT]), sb("keyT1", [P, G, GT])]
        relT = sb("relT", [P, G, GT])
        stage = sb("stage", [P, STG, 2, 1024])
        gath = sb("gath", [P, 2, GT, ROW])
        idx = sb("idx", [P, 2, GT], i32)
        onehot = sb("onehot", [P, GT, WIN])
        relw = sb("relw", [P, GT])
        iota = sb("iota", [P, WIN])
        ident = sb("ident", [P, P])
        before = sb("before", [P, P])
        rows = sb("rows", [1, 3, P], i32)
        gmm = sb("gmm", [P, 4])
        gmi = sb("gmi", [P, 1], i32)
        gmi2 = sb("gmi2", [P, 1], i32)
        coT = sb("coT", [NB, R[1]])
        co = sb("co", [R[1], NB])
        mean = sb("mean", [P, CH])
        var = sb("var", [P, CH])
        std = sb("std", [P, CH])
        rstd = sb("rstd", [P, CH])
        sq = sb("sq", [P, CH, D])
        rdeg = sb("rdeg", [P, CH])

        nat = stage[:, :, :, :].rearrange("p s t n -> p s (t n)")
        res = nat.rearrange("p s n -> p (s n)")[:, 0:TT * D].rearrange("p (t f) -> p t f", f=D)
        nat_i = [nat[0:G, a, :].bitcast(i32) for a in range(4)]
        nat_f = [nat[0:G, a, :] for a in range(4)]
        SRC, DST, T16, T32 = range(4)
        bas = accT[0:NB, 0:D * D]

        ps = ctx.enter_context(nc.psum_tensor("ps", [P, 8, 512], f32))
        ps_flat = ps[:, :, :].rearrange("p b n -> p (b n)")
        ps_acc = ps[0:D + 1, 0, 0:WIN]
        ps_hT = ps_flat[:, 6 * 512:6 * 512 + CH // 2 * P]
        ps_out = ps[:, 0:2, 0:480].rearrange("p b (t n) -> p b t n", n=96)

        s_padded = sem("s_padded")
        s_xzero = sem("s_xzero")
        s_x = sem("s_x")
        s_edges = sem("s_edges")
        s_w = sem("s_w")
        s_basis = sem("s_basis")
        s_w1copy = sem("s_w1copy")
        s_id0 = sem("s_id0")
        s_ident = sem("s_ident")
        s_const = sem("s_const")
        s_issue = sem("s_issue")
        s_dve = sem("s_dve")
        s_keys = sem("s_keys")
        s_gmm = sem("s_gmm")
        s_keyps = sem("s_keyps")
        s_keyev = sem("s_keyev")
        s_rowps = sem("s_rowps")
        s_rows = sem("s_rows")
        s_cops = sem("s_cops")
        s_coT = sem("s_coT")
        s_w1ps = sem("s_w1ps")
        s_w1 = sem("s_w1")
        s_ln = [sem("s_ln0"), sem("s_ln1")]
        s_var = [sem("s_var0"), sem("s_var1")]
        s_std = [sem("s_std0"), sem("s_std1")]
        s_h = [sem("s_h0"), sem("s_h1")]
        s_hTps = [sem("s_hTps0"), sem("s_hTps1")]
        s_hT = [sem("s_hT0"), sem("s_hT1")]
        s_prod = [sem("s_prod0"), sem("s_prod1")]
        s_staged = [sem("s_staged0"), sem("s_staged1")]
        s_store = [[sem(f"s_store{l}{b}") for b in range(STG)] for l in range(2)]
        s_idx = [sem("s_idx0"), sem("s_idx1")]
        s_gath = [[sem(f"s_gath{l}{b}") for b in range(2)] for l in range(2)]
        s_group = [sem("s_group0"), sem("s_group1")]
        s_relw = [sem("s_relw0"), sem("s_relw1")]
        s_hotstep = [sem("s_hotstep0"), sem("s_hotstep1")]
        s_hot = [sem("s_hot0"), sem("s_hot1")]
        s_sum = [sem("s_sum0"), sem("s_sum1")]
        s_acc = [sem("s_acc0"), sem("s_acc1")]
        s_accC = [sem("s_accC0"), sem("s_accC1")]
        s_outps = [sem("s_outps0"), sem("s_outps1")]
        s_outev = [sem("s_outev0"), sem("s_outev1")]
        s_selfps = sem("s_selfps")
        s_selfev = sem("s_selfev")
        s_base = sem("s_base")
        s_fin = sem("s_fin")
        s_final = sem("s_final")
        s_out = sem("s_out")

        class Chain:

            def __init__(self, eng, s, base=0):
                self.eng, self.s, self.base, self.n = eng, s, base, 0

            def step(self, ins):
                self.n += 1
                ins.then_inc(self.s, 1)
                self.eng.wait_ge(self.s, self.base + self.n)

        def chunk(t, c):
            return t[:, bass.ds(c * CH, CH), :]

        block = ctx.enter_context(nc.Block())

        @block.sync
        def _(sp):
            sp.wait_ge(s_padded, 4)
            for a, arr in ((SRC, src), (T16, type16), (DST, dst), (T32, type32)):
                t = nat_i[a]
                sp.dma_start(t[0:96, :], arr[0:96 * GE].rearrange("(g e) -> g e", e=GE)).then_inc(s_edges, 16)
                sp.dma_start(t[96:G - 1, :], arr[96 * GE:(G - 1) * GE].rearrange("(g e) -> g e", e=GE))\
                  .then_inc(s_edges, 16)
                sp.dma_start(t[G - 1:G, 0:LASTE], arr[(G - 1) * GE:E].rearrange("(g e) -> g e", g=1))\
                  .then_inc(s_edges, 16)
            for half in range(2):
                sp.dma_start(W[0][half * D:(half + 1) * D, :].rearrange("i (r o) -> i r o", r=R[0]),
                             weight0.rearrange("r i o -> i r o")).then_inc(s_w, 16)
                sp.dma_start(selfW[half * D:(half + 1) * D, :], self_weight).then_inc(s_w, 16)
            sp.dma_start(biasB[:, :], bias.rearrange("(a n) -> a n", a=1).broadcast_to([P, D])).then_inc(s_w, 16)
            sp.wait_ge(s_w1, 1)
            sp.dma_start(W[1][D:2 * D, :], W[1][0:D, :]).then_inc(s_w1copy, 16)

            for l in range(2):
                Q = R[l] * D // 512
                with sp.Fori(0, NCH) as c:
                    for u in range(UNITS[l]):
                        j, q = 2 * u // Q, 2 * u % Q
                        sp.wait_ge(s_staged[l], c * STEPS[l] + 2 * (u + 1))
                        sp.dma_start(table_v[l][:, bass.ds(c * CH + 2 * j, 2), q * 512:q * 512 + 1024],
                                     stage[:, u % STG, :, :]).then_inc(s_store[l][u % STG], 16)

            with sp.Fori(0, NCH) as c:
                sp.wait_ge(s_final, c + 1)
                for p0, p1 in ((0, SPLIT), (SPLIT, NP)):
                    sp.dma_start(out_v[p0:p1, bass.ds(c * (CH * D), CH * D)],
                                 res[p0:p1, bass.ds(c * CH, CH), :].rearrange("p t f -> p (t f)"))\
                      .then_inc(s_out, 16)
            sp.wait_ge(s_out, 32 * NCH)

        @block.gpsimd
        def _(pool):
            nc.gpsimd.memset(ident[:, :], 0.0).then_inc(s_id0, 1)
            nc.gpsimd.memset(before[:, :], 1.0).then_inc(s_id0, 1)
            pool.wait_ge(s_id0, 2)
            nc.gpsimd.affine_select(out=ident[:, :], in_=ident[:, :], compare_op=ALU.not_equal, fill=1.0, base=0,
                                    pattern=[[-1, P]], channel_multiplier=1).then_inc(s_ident, 1)
            nc.gpsimd.affine_select(out=before[:, :], in_=before[:, :], compare_op=ALU.is_gt, fill=0.0, base=0,
                                    pattern=[[1, P]], channel_multiplier=-1).then_inc(s_ident, 1)
            nc.gpsimd.iota(iota[:, :], [[1, WIN]], base=0, channel_multiplier=0,
                           allow_small_or_imprecise_dtypes=True).then_inc(s_const, 1)
            nc.gpsimd.memset(gath[:, :, :, :], 1.0).then_inc(s_const, 1)
            pool.wait_ge(s_const, 2)

            for l in range(2):
                def gather_group(b, tiles):
                    for c in range(tiles):
                        nc.gpsimd.indirect_dma_start(
                            out=gath[:, b, c, 0:D], out_offset=None, in_=table[l],
                            in_offset=bass.IndirectOffsetOnAxis(ap=idx[:, b, c:c + 1], axis=0))\
                            .then_inc(s_gath[l][b], 16)

                for b in range(STG):
                    pool.wait_ge(s_store[l][b], 16 * NCH * UNITS[l] // STG)
                for b in range(2):
                    pool.wait_ge(s_idx[l], b + 1)
                    gather_group(b, GT)
                with pool.Fori(1, G // 2 - 1) as i:
                    for b in range(2):
                        pool.wait_ge(s_group[l], i * 2 + (b - 1))
                        pool.wait_ge(s_idx[l], i * 2 + (b + 1))
                        pool.sem_inc(s_issue, 1)
                        gather_group(b, GT)
                for b in range(2):
                    pool.wait_ge(s_group[l], G - 3 + b)
                    pool.wait_ge(s_idx[l], G - 1 + b)
                    gather_group(b, GT if b == 0 else LASTT)

        @block.scalar
        def _(act):
            def copy_sums(l):
                last = act.value_load(rows[0:1, 1, G - 1:G], min_val=1, max_val=MAXW)
                before_last = act.value_load(rows[0:1, 2, G - 1:G], min_val=0, max_val=MAXW * G)
                act.wait_ge(s_acc[l], before_last + last + 1)

                def copy(c, first=False):
                    if not first:
                        act.wait_ge(s_outps[l], c)
                    nc.scalar.activation(accC[:, :, :], accT[:, :].rearrange("d (p t) -> d t p", t=TT)
                                         [:, bass.ds(c * CH, CH), :], ACT.Copy).then_inc(s_accC[l], 1)

                copy(0, first=True)
                with act.Fori(1, NCH) as c:
                    copy(c)

            act.dma_start(bas, basis.rearrange("b i o -> b (i o)")).then_inc(s_basis, 16)
            act.dma_start(co[:, :], coeff).then_inc(s_basis, 16)
            act.wait_ge(s_xzero, 1)
            for p0, p1 in ((0, SPLIT), (SPLIT, NP)):
                act.dma_start(xs[p0:p1, :, :].rearrange("p t f -> p (t f)"), x_v[p0:p1, :]).then_inc(s_x, 16)

            for l in range(2):
                Q = R[l] * D // 512
                per_slot = UNITS[l] // STG
                if l == 0:
                    act.wait_ge(s_keyev, 3)
                else:
                    copy_sums(0)
                    for b in range(STG):
                        act.wait_ge(s_store[0][b], 16 * NCH * UNITS[0] // STG)

                def std_of(c):
                    act.wait_ge(s_var[l], c + 1)
                    nc.scalar.activation(std[:, :], var[:, :], ACT.Sqrt).then_inc(s_std[l], 1)

                def dense_chunk(c, first=False, last=False):
                    act.wait_ge(s_hTps[l], c + 1)
                    nc.scalar.activation(hT[:, :, :], ps_hT.rearrange("p (j n) -> p j n", j=CP), ACT.Copy)\
                        .then_inc(s_hT[l], 1)
                    for k in range(STEPS[l]):
                        u = k // 2
                        if k % 2 == 0 and not (first and u < STG):
                            act.wait_ge(s_store[l][u % STG], c * (16 * per_slot) + 16 * (u // STG))
                        act.wait_ge(s_prod[l], c * STEPS[l] + (k + 1))
                        nc.scalar.activation(stage[:, u % STG, :, (k % 2) * 512:(k % 2) * 512 + 512],
                                             ps[:, 2 * (k % 2):2 * (k % 2) + 2, :], ACT.Copy)\
                            .then_inc(s_staged[l], 1)
                        if k == STEPS[l] // 2 and not last:
                            std_of(c + 1)

                std_of(0)
                dense_chunk(0, first=True)
                with act.Fori(1, NCH - 1) as c:
                    dense_chunk(c)
                dense_chunk(NCH - 1, last=True)

                def indices(g, b, gathers):
                    if gathers is not None:
                        act.wait_ge(s_gath[l][b], gathers * (16 * GT))
                    nc.scalar.activation(idx[:, b, :], keyT[l][:, bass.ds(g, 1), :]
                                         .rearrange("p a c -> p (a c)"), ACT.Copy).then_inc(s_idx[l], 1)

                if l == 1:
                    act.wait_ge(s_gath[0][0], 16 * GT * (G // 2))
                    act.wait_ge(s_gath[0][1], 16 * (GT * (G // 2 - 1) + LASTT))
                for b in range(2):
                    indices(b, b, None)
                with act.Fori(1, G // 2) as i:
                    for b in range(2):
                        indices(i * 2 + b, b, i)
            copy_sums(1)

        @block.tensor
        def _(pe):
            pe.wait_ge(s_ident, 2)
            pe.wait_ge(s_basis, 32)
            nc.tensor.transpose(ps[0:NB, 0, 0:R[1]], co[:, :], ident[0:R[1], 0:R[1]]).then_inc(s_cops, 1)
            pe.wait_ge(s_coT, 1)
            bas_v = bas.rearrange("b (i o) -> b o i", o=D)
            for o in range(D):
                last = nc.tensor.matmul(ps_flat[0:D, 2048 + o * R[1]:2048 + (o + 1) * R[1]], bas_v[:, o, :],
                                        coT[:, :], start=True, stop=True)
            last.then_inc(s_w1ps, 1)

            def turn_keys(nat_a, bank):
                for c in range(GT):
                    last = nc.tensor.transpose(ps_flat[:, bank * 512 + c * P:bank * 512 + c * P + G],
                                               nat_a[:, c * P:(c + 1) * P], ident[0:G, 0:G])
                last.then_inc(s_keyps, 1)

            pe.wait_ge(s_keys, 1)
            turn_keys(nat_f[T16], 0)
            pe.wait_ge(s_keys, 2)
            pe.wait_ge(s_w1, 1)
            turn_keys(nat_f[T32], 4)
            pe.wait_ge(s_keys, 3)
            pe.wait_ge(s_keyev, 1)
            turn_keys(nat_f[DST], 0)
            pe.wait_ge(s_keyev, 2)
            pe.wait_ge(s_gmm, 1)
            nc.tensor.matmul(ps[0:1, 4, 0:G], gmm[0:G, 1:2], ident[0:G, 0:G], start=True, stop=True)
            nc.tensor.matmul(ps[0:1, 4, P:P + G], gmm[0:G, 2:3], ident[0:G, 0:G], start=True, stop=True)
            nc.tensor.matmul(ps[0:1, 4, 2 * P:2 * P + G], gmm[0:G, 2:3], before[0:G, 0:G], start=True, stop=True)\
                .then_inc(s_rowps, 1)
            pe.wait_ge(s_keyev, 3)
            pe.wait_ge(s_rows, 1)

            def turn_sums(l):
                def turn(c, first=False):
                    pe.wait_ge(s_accC[l], c + 1)
                    if not first:
                        pe.wait_ge(s_outev[l], c)
                    for t in range(CH):
                        last = nc.tensor.transpose(ps_out[:, t // 5, t % 5, 0:D + 1], accC[:, t, :],
                                                   ident[0:D + 1, 0:D + 1])
                    last.then_inc(s_outps[l], 1)

                turn(0, first=True)
                with pe.Fori(1, NCH) as c:
                    turn(c)

            for l in range(2):
                if l == 0:
                    pe.wait_ge(s_w, 16 * 5)
                else:
                    turn_sums(0)
                    pe.wait_ge(s_w1copy, 16)
                    pe.wait_ge(s_outev[0], NCH)

                def dense_chunk(c, first):
                    pe.wait_ge(s_h[l], c + 1)
                    for j in range(CP):
                        last = nc.tensor.transpose(ps_hT[:, j * P:(j + 1) * P],
                                                   h[:, 2 * j:2 * j + 2, :].rearrange("p t f -> p (t f)"),
                                                   ident[:, :])
                    last.then_inc(s_hTps[l], 1)
                    pe.wait_ge(s_hT[l], c + 1)
                    if l == 1:
                        if not first:
                            pe.wait_ge(s_selfev, c)
                        for j in range(CP):
                            for half in range(2):
                                part = slice(half * D, (half + 1) * D)
                                last = nc.tensor.matmul(ps[:, 4 + half, j * D:(j + 1) * D], hT[part, j, :],
                                                        selfW[part, :], start=True, stop=True)
                        last.then_inc(s_selfps, 1)
                    for k in range(STEPS[l]):
                        j, q = divmod(k, R[l] * D // 512)
                        if not (first and k < 2):
                            pe.wait_ge(s_staged[l], c * STEPS[l] + (k - 1))
                        for half in range(2):
                            part = slice(half * D, (half + 1) * D)
                            last = nc.tensor.matmul(ps[:, 2 * (k % 2) + half, :], hT[part, j, :],
                                                    W[l][part, q * 512:(q + 1) * 512], start=True, stop=True)
                        last.then_inc(s_prod[l], 1)

                dense_chunk(0, True)
                with pe.Fori(1, NCH) as c:
                    dense_chunk(c, False)
                pe.wait_ge(s_staged[l], NCH * STEPS[l])

                def sum_group(g, b, gathers, tiles):
                    pe.wait_ge(s_gath[l][b], gathers)
                    windows = pe.value_load(rows[0:1, 1, bass.ds(g, 1)], min_val=1, max_val=MAXW)
                    done = pe.value_load(rows[0:1, 2, bass.ds(g, 1)], min_val=0, max_val=MAXW * G)
                    with pe.Fori(0, windows) as w:
                        pe.wait_ge(s_hot[l], done + w + 1)
                        for c in range(tiles):
                            last = nc.tensor.matmul(ps_acc, gath[:, b, c, 0:D + 1], onehot[:, c, :],
                                                    start=(c == 0), stop=(c == tiles - 1))
                        last.then_inc(s_sum[l], 1)
                    pe.wait_ge(s_sum[l], done + windows)
                    pe.nop().then_inc(s_group[l], 1)

                with pe.Fori(0, G // 2 - 1) as i:
                    for b in range(2):
                        sum_group(i * 2 + b, b, (i + 1) * (16 * GT), GT)
                sum_group(G - 2, 0, 16 * GT * (G // 2), GT)
                sum_group(G - 1, 1, 16 * (GT * (G // 2 - 1) + LASTT), LASTT)

            turn_sums(1)

        @block.vector
        def _(dve):
            dve_chain = Chain(dve, s_dve)
            for a in range(4):
                nc.vector.memset(nat_i[a][96:G, :], NO_NODE if a == DST else 0).then_inc(s_padded, 1)
            nc.vector.memset(xs[:, :, :], 0.0).then_inc(s_xzero, 1)

            def wide(v):
                return v[:, :].rearrange("p (t a) -> p t a", a=1).broadcast_to([P, CH, D])

            def ln_stats(l, c, first=False):
                ch = Chain(dve, s_ln[l], c * 6)
                hc = h[:, :, :]
                if not first:
                    dve.wait_ge(s_hTps[l], c)
                ch.step(nc.vector.tensor_reduce(out=mean[:, :], in_=chunk(xs, c), axis=AX.X, op=ALU.add))
                ch.step(nc.vector.tensor_scalar(mean[:, :], mean[:, :], 1.0 / D, None, ALU.mult))
                ch.step(nc.vector.tensor_tensor(hc, chunk(xs, c), wide(mean), ALU.subtract))
                ch.step(nc.vector.tensor_tensor(sq[:, :, :], hc, hc, ALU.mult))
                ch.step(nc.vector.tensor_reduce(out=var[:, :], in_=sq[:, :, :], axis=AX.X, op=ALU.add))
                nc.vector.tensor_scalar(var[:, :], var[:, :], 1.0 / D, EPS, ALU.mult, ALU.add)\
                    .then_inc(s_var[l], 1)

            def ln_scale(l, c):
                ch = Chain(dve, s_ln[l], c * 6 + 5)
                dve.wait_ge(s_std[l], c + 1)
                ch.step(nc.vector.reciprocal(rstd[:, :], std[:, :]))
                nc.vector.scalar_tensor_tensor(h[:, :, :], h[:, :, :], 0.0, wide(rstd), ALU.max, ALU.mult)\
                    .then_inc(s_h[l], 1)

            dve.wait_ge(s_cops, 1)
            nc.vector.tensor_copy(coT[:, :], ps[0:NB, 0, 0:R[1]]).then_inc(s_coT, 1)
            dve.wait_ge(s_w1ps, 1)
            nc.vector.tensor_copy(W[1][0:D, :].rearrange("i (r o) -> i r o", r=R[1]),
                                  ps_flat[0:D, 2048:4096].rearrange("i (o r) -> i r o", r=R[1])).then_inc(s_w1, 1)

            dve.wait_ge(s_edges, 16 * 12)
            nc.vector.scalar_tensor_tensor(nat_f[T16], nat_i[SRC], float(R[0]), nat_i[T16], ALU.mult, ALU.add)\
                .then_inc(s_keys, 1)
            nc.vector.scalar_tensor_tensor(nat_f[T32], nat_i[SRC], float(R[1]), nat_i[T32], ALU.mult, ALU.add)\
                .then_inc(s_keys, 1)
            dve.wait_ge(s_keys, 2)
            real = nat_f[SRC]
            dve_chain.step(nc.vector.tensor_copy(nat_f[DST], nat_i[DST]))
            dve_chain.step(nc.vector.tensor_reduce(out=gmm[0:G, 0:1], in_=nat_f[DST], axis=AX.X, op=ALU.max))
            dve_chain.step(nc.vector.tensor_scalar(real, nat_f[DST], 0.0, 1.0e6, ALU.is_lt, ALU.mult))
            dve_chain.step(nc.vector.tensor_tensor(real, real, nat_f[DST], ALU.add))
            dve_chain.step(nc.vector.tensor_reduce(out=gmm[0:G, 1:2], in_=real, axis=AX.X, op=ALU.min))
            nc.vector.tensor_scalar(nat_f[DST], nat_f[DST], gmm[0:G, 1:2], None, ALU.subtract).then_inc(s_keys, 1)
            dve_chain.step(nc.vector.tensor_tensor(gmi[0:G, :], gmm[0:G, 0:1], gmm[0:G, 1:2], ALU.subtract))
            dve_chain.step(nc.vector.tensor_scalar(gmi2[0:G, :], gmi[0:G, :], 7, None, ALU.arith_shift_right))
            nc.vector.tensor_scalar(gmm[0:G, 2:3], gmi2[0:G, :], 1.0, None, ALU.add).then_inc(s_gmm, 1)
            for n, (t, bank) in enumerate(((keyT[0], 0), (keyT[1], 4), (relT, 0))):
                dve.wait_ge(s_keyps, n + 1)
                nc.vector.tensor_copy(t[:, :, :], ps_flat[:, bank * 512:bank * 512 + GT * P]
                                      .rearrange("p (c g) -> p g c", c=GT)[:, 0:G, :]).then_inc(s_keyev, 1)
            dve.wait_ge(s_rowps, 1)
            nc.vector.tensor_copy(rows[:, :, 0:G], ps[0:1, 4, 0:3 * P].rearrange("p (a g) -> p a g", a=3)[:, :, 0:G])\
                .then_inc(s_rows, 1)
            dve.wait_ge(s_xzero, 1)
            dve.wait_ge(s_x, 32)
            ln_stats(0, 0, first=True)
            with dve.Fori(0, NCH - 1) as c:
                ln_scale(0, c)
                ln_stats(0, c + 1)
            ln_scale(0, NCH - 1)

            for l in range(2):
                if l == 1:
                    def add_sums(c):
                        dve.wait_ge(s_outps[0], c + 1)
                        nc.vector.tensor_tensor(chunk(xs, c).rearrange("p (b t) f -> p b t f", b=2),
                                                chunk(xs, c).rearrange("p (b t) f -> p b t f", b=2),
                                                ps_out[:, :, :, 0:D], ALU.add).then_inc(s_outev[0], 1)

                    with dve.Fori(0, NCH) as c:
                        add_sums(c)
                    dve.wait_ge(s_outev[0], NCH)
                    def add_self(c):
                        dve.wait_ge(s_selfps, c + 1)
                        by_half = chunk(xs, c).rearrange("p (j a) f -> p a j f", a=2)
                        nc.vector.tensor_tensor(by_half, by_half, ps[:, 4:6, 0:CP * D]
                                                .rearrange("p a (j f) -> p a j f", f=D), ALU.add)\
                            .then_inc(s_selfev, 1)
                        dve.wait_ge(s_selfev, c + 1)
                        nc.vector.tensor_tensor(chunk(xs, c), chunk(xs, c),
                                                biasB[:, :].rearrange("p (a f) -> p a f", a=1)
                                                .broadcast_to([P, CH, D]), ALU.add).then_inc(s_base, 1)

                    ln_stats(1, 0, first=True)
                    with dve.Fori(0, NCH - 1) as c:
                        ln_scale(1, c)
                        add_self(c)
                        ln_stats(1, c + 1)
                    ln_scale(1, NCH - 1)
                    add_self(NCH - 1)
                if l == 1:
                    dve.wait_ge(s_accC[0], NCH)
                else:
                    dve.wait_ge(s_w1ps, 1)
                nc.vector.memset(accT[:, :], 0.0).then_inc(s_acc[l], 1)
                nc.vector.memset(relw[:, :], 0.0).then_inc(s_hotstep[l], 1)
                dve.wait_ge(s_rows, 1)
                dve.wait_ge(s_keyev, 3)
                dve.wait_ge(s_const, 2)

                with dve.Fori(0, G) as g:
                    base = dve.value_load(rows[0:1, 0, bass.ds(g, 1)], min_val=0, max_val=N - 1)
                    windows = dve.value_load(rows[0:1, 1, bass.ds(g, 1)], min_val=1, max_val=MAXW)
                    done = dve.value_load(rows[0:1, 2, bass.ds(g, 1)], min_val=0, max_val=MAXW * G)
                    dve.wait_ge(s_hotstep[l], done + 1)
                    nc.vector.tensor_copy(relw[:, :], relT[:, bass.ds(g, 1), :].rearrange("p a c -> p (a c)"))\
                        .then_inc(s_relw[l], 1)
                    with dve.Fori(0, windows) as w:
                        dve.wait_ge(s_relw[l], g + 1)
                        dve.wait_ge(s_hotstep[l], done + w + 1)
                        nc.vector.tensor_tensor(onehot[:, :, :],
                                                iota[:, :].rearrange("p (a n) -> p a n", a=1).broadcast_to([P, GT, WIN]),
                                                relw[:, :].rearrange("p (c a) -> p c a", a=1).broadcast_to([P, GT, WIN]),
                                                ALU.is_equal).then_inc(s_hot[l], 1)
                        dve.wait_ge(s_hot[l], done + w + 1)
                        nc.vector.tensor_scalar(relw[:, :], relw[:, :], float(-WIN), None, ALU.add)\
                            .then_inc(s_hotstep[l], 1)
                        dve.wait_ge(s_sum[l], done + w + 1)
                        dve.wait_ge(s_acc[l], done + w + 1)
                        start = nc.s_assert_within(base + w * WIN, 0, N - 1)
                        win = accT[:, bass.ds(start, WIN)]
                        nc.vector.tensor_tensor(win, win, ps_acc, ALU.add).then_inc(s_acc[l], 1)

            dve.wait_ge(s_base, NCH)
            for b in range(STG):
                dve.wait_ge(s_store[1][b], 16 * NCH * UNITS[1] // STG)
            with dve.Fori(0, NCH) as c:
                ch = Chain(dve, s_fin, c * 2)
                dve.wait_ge(s_outps[1], c + 1)
                deg4 = rdeg[:, :].rearrange("p (b t a) -> p b t a", b=2, a=1)
                ch.step(nc.vector.tensor_scalar(deg4, ps_out[:, :, :, D:D + 1], 1.0, None, ALU.max))
                ch.step(nc.vector.reciprocal(rdeg[:, :], rdeg[:, :]))
                h4 = chunk(res, c).rearrange("p (b t) f -> p b t f", b=2)
                nc.vector.tensor_tensor(h4, ps_out[:, :, :, 0:D], deg4.broadcast_to([P, 2, 5, D]), ALU.mult)\
                    .then_inc(s_outev[1], 1)
                dve.wait_ge(s_outev[1], c + 1)
                nc.vector.tensor_tensor(chunk(res, c), chunk(res, c), chunk(xs, c), ALU.add).then_inc(s_final, 1)


_INS = ["x", "src", "dst", "edge_type_16", "edge_type_32", "L0_gnn_weight", "L1_gnn_basis", "L1_gnn_coeff",
        "L1_gnn_self_weight", "L1_gnn_bias"]


def kernel(**inputs):
    import numpy as np
    import concourse.bacc as bacc
    from concourse import mybir as mb
    from concourse.bass_utils import run_bass_kernel_spmd

    nc = bacc.Bacc("TRN2", target_bir_lowering=False, num_devices=1)
    arrays, args = {}, []
    for name in _INS:
        a = np.ascontiguousarray(inputs[name])
        arrays[f"in_{name}"] = a
        args.append(nc.dram_tensor(f"in_{name}", a.shape, mb.dt.from_np(a.dtype), kind="ExternalInput").ap())
    shape = arrays["in_x"].shape
    args.append(nc.dram_tensor("out_x", shape, mb.dt.float32, kind="ExternalOutput").ap())
    two_layer_gnn_kernel(nc, *args)
    r = run_bass_kernel_spmd(nc, [arrays], core_ids=[0])
    return r.results[0]["out_x"]
```

```python
import concourse.bass as bass
from concourse import mybir
from contextlib import ExitStack


def two_layer_gnn_kernel(nc, x, src, dst, type16, type32, weight0, basis, coeff, self_weight, bias, out):
    f32, i32 = mybir.dt.float32, mybir.dt.int32
    ALU, ACT, AX = mybir.AluOpType, mybir.ActivationFunctionType, mybir.AxisListType

    N, D = x.shape
    E = src.shape[0]
    R = (weight0.shape[0], coeff.shape[0])
    NB = basis.shape[0]
    P = 128
    D1 = D + 1
    TT = 50
    NP = N // TT
    assert NP * TT == N and NP <= P
    CH = 10
    NCH = TT // CH
    CP = CH // 2
    GT = 16
    GE = GT * P
    G = -(-E // GE)
    assert G % 2 == 0
    LASTE = E - (G - 1) * GE
    LASTT = -(-LASTE // P)
    NW = P // GT
    KEYS = [NW * R[l] for l in range(2)]
    COLS = 128
    HALVES = [KEYS[l] // COLS for l in range(2)]
    RC = COLS // NW
    M = [D1, D]
    MP = [D1, 2 * D]
    assert HALVES == [1, 2]
    BANKT = 4
    UNITS = GT // BANKT
    HB = 4
    SPAN = P
    MAXW = (N - 1) // NW + 1
    MAXV = (N - 1) // SPAN + 1
    VBITS = MAXV.bit_length()
    ROW = 80
    NO_EDGE = -1000000
    EPS = 1e-5

    table = [nc.dram_tensor(f"table{l}", (P * TT, D), f32, kind="Internal").ap() for l in range(2)]
    table_v = [table[l].rearrange("(p t) f -> p (t f)", p=P) for l in range(2)]
    x_v = x.rearrange("(p t) f -> p (t f)", t=TT)
    out_v = out.rearrange("(p t) f -> p (t f)", t=TT)

    ctx = ExitStack()
    with ctx:
        def sb(name, shape, dt=f32):
            return ctx.enter_context(nc.sbuf_tensor(name, shape, dt))

        def sem(name):
            return ctx.enter_context(nc.semaphore(name))

        def sems(name):
            return [sem(f"{name}{l}") for l in range(2)]

        xs = sb("xs", [P, TT, D])
        h = sb("h", [P, TT, D])
        hc = sb("hc", [P, CH, D])
        hT = sb("hT", [P, CP, P])
        accT = sb("accT", [D1, P * TT])
        accC = sb("accC", [D1, CH, P])
        W = [sb("W0", [D1, R[0], D1]), sb("W1", [P, RC, D])]
        selfW = sb("selfW", [P, D])
        biasB = sb("biasB", [P, 1, D])
        srcT = sb("srcT", [P, G, GT])
        keyT = [sb(f"keyT{l}", [P, G + 1, GT]) for l in range(2)]
        gath = sb("gath", [P, 2, GT, ROW])
        idx = sb("idx", [P, 2, GT], i32)
        onehot = sb("onehot", [P, 2, 2048])
        agg = sb("agg", [P, RC, GT, NW])
        natx = sb("natx", [P, 2048])
        keyw = sb("keyw", [P, GT])
        iotaK = [sb(f"iotaK{l}", [P, HALVES[l], RC, NW]) for l in range(2)]
        iotaS = sb("iotaS", [P, SPAN])
        slot = sb("slot", [P, G])
        slotw = sb("slotw", [P, 1])
        slotv = sb("slotv", [P, 1])
        slothot = sb("slothot", [P, SPAN])
        y = sb("y", [P, D1])
        ident = sb("ident", [P, P])
        rep = sb("rep", [GT, P])
        rowf = sb("rowf", [1, 3, P])
        rows = sb("rows", [1, 3, P], i32)
        BASE, WINS, SPANS = range(3)
        COUNTS = 1
        tmin = sb("tmin", [P, GT])
        tmax = sb("tmax", [P, GT])
        trel = sb("trel", [P, GT])
        tminT = sb("tminT", [GT, P])
        gm = sb("gm", [P, 8])
        GMIN, GMAX, GW, GV = range(4)
        gi = sb("gi", [P, 2], i32)
        gj = sb("gj", [P, 2], i32)
        lane = sb("lane", [P, 1], i32)
        lane8i = sb("lane8i", [P, 1], i32)
        lane8 = sb("lane8", [P, 1])
        coT = sb("coT", [NB, R[1]])
        co = sb("co", [R[1], NB])
        mean = sb("mean", [P, CH])
        var = sb("var", [P, CH])
        std = sb("std", [P, CH])
        rstd = sb("rstd", [P, CH])
        sq = sb("sq", [P, CH, D])
        rdeg = sb("rdeg", [P, TT])

        nat = [onehot[0:G, 0, :], agg[0:G, :, :, :].rearrange("p r c n -> p (r c n)"), onehot[0:G, 1, :],
               natx[0:G, :]]
        nat_i = [t.bitcast(i32) for t in nat]
        SRC, DST, T16, T32 = range(4)
        bas = accT[0:NB, 0:D * D]
        hot_v = [onehot[:, :, :].rearrange("p a n -> p (a n)")[:, 0:GT * KEYS[l]]
                 .rearrange("p (c k) -> p c k", c=GT) for l in range(2)]

        ps = ctx.enter_context(nc.psum_tensor("ps", [P, 8, 512], f32))
        ps_flat = ps[:, :, :].rearrange("p b n -> p (b n)")
        ps_y = [ps[:, 4, 0:M[l]] for l in range(2)]
        ps_acc = [ps[0:M[l], 5, 0:SPAN] for l in range(2)]
        ps_hT = ps_flat[:, 6 * 512:6 * 512 + CP * P]
        ps_out = ps[:, 0:2, 0:480].rearrange("p b (t n) -> p b t n", n=96)
        ps_self = ps[:, 2:4, 0:CP * D]

        s_pad = sem("s_pad")
        s_xzero = sem("s_xzero")
        s_x = sem("s_x")
        s_src = sem("s_src")
        s_edges = sem("s_edges")
        s_wzero = sem("s_wzero")
        s_w = sem("s_w")
        s_basis = sem("s_basis")
        s_id0 = sem("s_id0")
        s_ident = sem("s_ident")
        s_rep = sem("s_rep")
        s_lane = sem("s_lane")
        s_const = sem("s_const")
        s_issue = sem("s_issue")
        s_srcf = sem("s_srcf")
        s_srcps = sem("s_srcps")
        s_srcT = sem("s_srcT")
        s_setup = sem("s_setup")
        s_keys = sem("s_keys")
        s_keyps = sem("s_keyps")
        s_keyT = sem("s_keyT")
        s_gm = sem("s_gm")
        s_tminps = sem("s_tminps")
        s_tminT = sem("s_tminT")
        s_rowps = sem("s_rowps")
        s_rows = sem("s_rows")
        s_cops = sem("s_cops")
        s_coT = sem("s_coT")
        s_w1ps = sem("s_w1ps")
        s_w1 = sem("s_w1")
        s_ln, s_var, s_std, s_h = sems("s_ln"), sems("s_var"), sems("s_std"), sems("s_h")
        s_store = sems("s_store")
        s_hc, s_hTps, s_hT, s_selfps, s_self = [sem(n) for n in ("s_hc", "s_hTps", "s_hT", "s_selfps", "s_self")]
        s_idx = sems("s_idx")
        s_gath = [[sem(f"s_gath{l}{b}") for b in range(2)] for l in range(2)]
        s_group = sems("s_group")
        s_keyw = sems("s_keyw")
        s_hot = sems("s_hot")
        s_tiles = sems("s_tiles")
        s_agg = sems("s_agg")
        s_yps = sems("s_yps")
        s_y = sems("s_y")
        s_slotw = sems("s_slotw")
        s_slotv = sems("s_slotv")
        s_slothot = sems("s_slothot")
        s_spanstep = sems("s_spanstep")
        s_span = sems("s_span")
        s_acc = sems("s_acc")
        s_keypad = sem("s_keypad")
        s_rowf = sem("s_rowf")
        s_accC, s_outps, s_outev = sems("s_accC"), sems("s_outps"), sems("s_outev")
        s_base = sem("s_base")
        s_xsum = sem("s_xsum")
        s_final = sem("s_final")
        s_out = sem("s_out")

        class Chain:

            def __init__(self, eng, s, base=0):
                self.eng, self.s, self.base, self.n = eng, s, base, 0

            def step(self, ins):
                self.n += 1
                ins.then_inc(self.s, 1)
                self.eng.wait_ge(self.s, self.base + self.n)

        def chunk(t, c):
            return t[:, bass.ds(c * CH, CH), :]

        class Count:

            def __init__(self, eng, name, high):
                self.eng, self.reg, self.high = eng, eng.alloc_register(name), high

            def zero(self):
                self.eng.reg_mov(self.reg, 0)

            def add(self, n):
                self.eng.reg_add(self.reg, self.reg, n)

            def value(self):
                return self.eng.snap(self.reg, min_val=0, max_val=self.high)

        def group_counts(eng, g):
            both = eng.value_load(rows[0:1, COUNTS, bass.ds(g, 1)], min_val=0, max_val=MAXW << VBITS | MAXV)
            wins = eng.snap(both >> VBITS, min_val=1, max_val=MAXW)
            spans = eng.snap(both & ((1 << VBITS) - 1), min_val=1, max_val=MAXV)
            return wins, spans

        block = ctx.enter_context(nc.Block())

        @block.sync
        def _(sp):
            sp.dma_start(xs[0:96, :, :].rearrange("p t f -> p (t f)"), x_v[0:96, :]).then_inc(s_x, 16)
            sp.wait_ge(s_xzero, 1)
            for p0, p1 in ((96, 112), (112, NP)):
                sp.dma_start(xs[p0:p1, :, :].rearrange("p t f -> p (t f)"), x_v[p0:p1, :]).then_inc(s_x, 16)
            sp.wait_ge(s_pad, 4)
            for a, arr, s in ((DST, dst, s_edges), (T16, type16, s_edges), (T32, type32, s_edges)):
                t = nat_i[a]
                sp.dma_start(t[0:96, :], arr[0:96 * GE].rearrange("(g e) -> g e", e=GE)).then_inc(s, 16)
                sp.dma_start(t[96:G - 1, :], arr[96 * GE:(G - 1) * GE].rearrange("(g e) -> g e", e=GE))\
                  .then_inc(s, 16)
                sp.dma_start(t[G - 1:G, 0:LASTE], arr[(G - 1) * GE:E].rearrange("(g e) -> g e", g=1))\
                  .then_inc(s, 16)

            sp.dma_start(nat_i[DST][G - 1:G, LASTE:GE], dst[E - (GE - LASTE):E].rearrange("(g e) -> g e", g=1))\
              .then_inc(s_edges, 16)

            for l in range(2):
                with sp.Fori(0, NCH) as c:
                    sp.wait_ge(s_h[l], c + 1)
                    sp.dma_start(table_v[l][:, bass.ds(c * (CH * D), CH * D)],
                                 chunk(h, c).rearrange("p t f -> p (t f)")).then_inc(s_store[l], 16)

            with sp.Fori(0, NCH) as c:
                sp.wait_ge(s_final, c + 1)
                for p0, p1 in ((0, 112), (112, NP)):
                    sp.dma_start(out_v[p0:p1, bass.ds(c * (CH * D), CH * D)],
                                 h[p0:p1, bass.ds(c * CH, CH), :].rearrange("p t f -> p (t f)"))\
                      .then_inc(s_out, 16)
            sp.wait_ge(s_out, 32 * NCH)

        @block.gpsimd
        def _(pool):
            nc.gpsimd.memset(ident[:, :], 0.0).then_inc(s_id0, 1)
            nc.gpsimd.memset(rep[:, :], 1.0).then_inc(s_id0, 1)
            pool.wait_ge(s_id0, 2)
            nc.gpsimd.affine_select(out=ident[:, :], in_=ident[:, :], compare_op=ALU.not_equal, fill=1.0, base=0,
                                    pattern=[[-1, P]], channel_multiplier=1).then_inc(s_ident, 1)
            nc.gpsimd.affine_select(out=rep[:, :], in_=rep[:, :], compare_op=ALU.is_ge, fill=0.0, base=0,
                                    pattern=[[1, P]], channel_multiplier=-NW).then_inc(s_rep, 1)
            pool.wait_ge(s_rep, 1)
            nc.gpsimd.affine_select(out=rep[:, :], in_=rep[:, :], compare_op=ALU.is_ge, fill=0.0, base=NW - 1,
                                    pattern=[[-1, P]], channel_multiplier=NW).then_inc(s_rep, 1)
            nc.gpsimd.iota(lane[:, :], [[0, 1]], base=0, channel_multiplier=1).then_inc(s_lane, 1)
            for l in range(2):
                nc.gpsimd.iota(iotaK[l][:, :, :, :], [[RC, HALVES[l]], [1, RC], [R[l], NW]], base=0, channel_multiplier=0,
                               allow_small_or_imprecise_dtypes=True).then_inc(s_const, 1)
            nc.gpsimd.iota(iotaS[:, :], [[1, SPAN]], base=0, channel_multiplier=0,
                           allow_small_or_imprecise_dtypes=True).then_inc(s_const, 1)
            nc.gpsimd.memset(gath[:, :, :, :], 1.0).then_inc(s_const, 1)
            pool.wait_ge(s_const, 4)

            for l in range(2):
                def gather_group(b, tiles):
                    for c in range(tiles):
                        nc.gpsimd.indirect_dma_start(
                            out=gath[:, b, c, 0:D], out_offset=None, in_=table[l],
                            in_offset=bass.IndirectOffsetOnAxis(ap=idx[:, b, c:c + 1], axis=0))\
                            .then_inc(s_gath[l][b], 16)

                pool.wait_ge(s_store[l], 16 * NCH)
                for b in range(2):
                    pool.wait_ge(s_idx[l], b + 1)
                    gather_group(b, GT)

                def gather_again(g, b, tiles):
                    pool.wait_ge(s_group[l], g - 1)
                    pool.wait_ge(s_idx[l], g + 1)
                    pool.sem_inc(s_issue, 1)
                    gather_group(b, tiles)

                with pool.Fori(1, G // 2 - 1) as i:
                    for b in range(2):
                        gather_again(i * 2 + b, b, GT)
                gather_again(G - 2, 0, GT)
                gather_again(G - 1, 1, LASTT)

        @block.scalar
        def _(act):
            act.wait_ge(s_pad, 1)
            act.dma_start(nat_i[SRC][0:96, :], src[0:96 * GE].rearrange("(g e) -> g e", e=GE)).then_inc(s_src, 16)
            act.dma_start(nat_i[SRC][96:G - 1, :], src[96 * GE:(G - 1) * GE].rearrange("(g e) -> g e", e=GE))\
               .then_inc(s_src, 16)
            act.dma_start(nat_i[SRC][G - 1:G, 0:LASTE], src[(G - 1) * GE:E].rearrange("(g e) -> g e", g=1))\
               .then_inc(s_src, 16)
            act.dma_start(bas, basis.rearrange("b i o -> b (i o)")).then_inc(s_basis, 16)
            act.dma_start(co[:, :], coeff).then_inc(s_basis, 16)
            act.wait_ge(s_wzero, 2)
            act.dma_start(W[0][0:D, :, 0:D], weight0.rearrange("r i o -> i r o")).then_inc(s_w, 16)
            for half in range(2):
                act.dma_start(selfW[half * D:(half + 1) * D, :], self_weight).then_inc(s_w, 16)
            act.dma_start(biasB[:, 0, :], bias.rearrange("(a n) -> a n", a=1).broadcast_to([P, D]))\
               .then_inc(s_w, 16)

            act_wins = Count(act, "act_wins", MAXW * G)
            act_spans = Count(act, "act_spans", MAXW * MAXV * G)

            def std_of(l, c):
                act.wait_ge(s_var[l], c + 1)
                nc.scalar.activation(std[:, :], var[:, :], ACT.Sqrt).then_inc(s_std[l], 1)

            def copy_sums(l):
                act.wait_ge(s_acc[l], act_spans.value() + 1)

                def copy(c, first=False):
                    if not first:
                        act.wait_ge(s_outps[l], c)
                    nc.scalar.activation(accC[:, :, :], accT[:, :].rearrange("d (p t) -> d t p", t=TT)
                                         [:, bass.ds(c * CH, CH), :], ACT.Copy).then_inc(s_accC[l], 1)

                copy(0, first=True)
                with act.Fori(1, NCH) as c:
                    copy(c)

            std_of(0, 0)
            act.wait_ge(s_src, 48)
            nc.scalar.activation(nat[SRC], nat_i[SRC], ACT.Copy).then_inc(s_srcf, 1)
            with act.Fori(1, NCH) as c:
                std_of(0, c)
            act.wait_ge(s_srcps, 1)
            nc.scalar.activation(srcT[:, :, :], ps_flat[:, 0:GT * P].rearrange("p (c g) -> p g c", c=GT)[:, 0:G, :],
                                 ACT.Copy).then_inc(s_srcT, 1)

            for l in range(2):
                if l == 1:
                    def self_chunk(c, first=False):
                        if not first:
                            act.wait_ge(s_hTps, c)
                        act.wait_ge(s_h[1], c + 1)
                        nc.scalar.activation(hc[:, :, :], chunk(h, c), ACT.Copy).then_inc(s_hc, 1)
                        act.wait_ge(s_hTps, c + 1)
                        if not first:
                            act.wait_ge(s_selfps, c)
                        nc.scalar.activation(hT[:, :, :], ps_hT.rearrange("p (j n) -> p j n", j=CP), ACT.Copy)\
                            .then_inc(s_hT, 1)

                    copy_sums(0)
                    std_of(1, 0)
                    std_of(1, 1)
                    self_chunk(0, first=True)
                    with act.Fori(1, NCH - 1) as c:
                        std_of(1, c + 1)
                        self_chunk(c)

                def senders(g, b, gathers):
                    if gathers is not None:
                        act.wait_ge(s_gath[l][b], gathers)
                    nc.scalar.activation(idx[:, b, :], srcT[:, bass.ds(g, 1), :].rearrange("p a c -> p (a c)"),
                                         ACT.Copy).then_inc(s_idx[l], 1)

                def aggregates(g):
                    wins, spans = group_counts(act, g)
                    with act.Fori(0, wins):
                        k = act_wins.value()
                        for u in range(UNITS):
                            if u == 0:
                                act.wait_ge(s_y[l], k + 1)
                            act.wait_ge(s_tiles[l], k * UNITS + (u + 1))
                            nc.scalar.activation(agg[0:MP[l], :, u * BANKT:(u + 1) * BANKT, :]
                                                 .rearrange("p r c n -> p c r n"),
                                                 ps[0:MP[l], u, :].rearrange("p (c r n) -> p c r n", c=BANKT, r=RC),
                                                 ACT.Copy).then_inc(s_agg[l], 1)
                        act_wins.add(1)
                        act_spans.add(spans)

                act.wait_ge(s_srcT, 1)
                if l == 1:
                    act.wait_ge(s_gath[0][0], 16 * GT * (G // 2))
                    act.wait_ge(s_gath[0][1], 16 * (GT * (G // 2 - 1) + LASTT))
                for b in range(2):
                    senders(b, b, None)
                if l == 1:
                    self_chunk(NCH - 1)
                act.wait_ge(s_rows, 3)
                act.wait_ge(s_keyT, 2)
                act.sem_inc(s_agg[l], UNITS)
                act_wins.zero()
                act_spans.zero()
                with act.Fori(0, G // 2 - 1) as i:
                    for b in range(2):
                        senders(i * 2 + (b + 2), b, (i + 1) * (16 * GT))
                        aggregates(i * 2 + b)
                for g in range(G - 2, G):
                    aggregates(g)

            copy_sums(1)

        @block.tensor
        def _(pe):
            pe_wins = Count(pe, "pe_wins", MAXW * G)
            pe_spans = Count(pe, "pe_spans", MAXW * MAXV * G)

            def turn_edges(a, bank, done):
                for c in range(GT):
                    last = nc.tensor.transpose(ps_flat[:, bank * 512 + c * P:bank * 512 + c * P + G],
                                               nat[a][:, c * P:(c + 1) * P], ident[0:G, 0:G])
                last.then_inc(done, 1)

            pe.wait_ge(s_ident, 1)
            pe.wait_ge(s_srcf, 1)
            turn_edges(SRC, 0, s_srcps)
            pe.wait_ge(s_basis, 32)
            nc.tensor.transpose(ps[0:NB, 4, 0:R[1]], co[:, :], ident[0:R[1], 0:R[1]]).then_inc(s_cops, 1)
            pe.wait_ge(s_coT, 1)
            bas_v = bas.rearrange("b (i o) -> b o i", o=D)
            for o in range(D):
                for half in range(2):
                    last = nc.tensor.matmul(ps_flat[half * D:(half + 1) * D, 2048 + o * RC:2048 + (o + 1) * RC],
                                            bas_v[:, o, :], coT[:, half * RC:(half + 1) * RC], start=True, stop=True)
            last.then_inc(s_w1ps, 1)
            pe.wait_ge(s_keys, 1)
            pe.wait_ge(s_srcT, 1)
            turn_edges(T16, 0, s_keyps)
            pe.wait_ge(s_keys, 2)
            pe.wait_ge(s_w1, 1)
            turn_edges(T32, 4, s_keyps)
            pe.wait_ge(s_gm, 1)
            pe.wait_ge(s_keyT, 1)
            nc.tensor.transpose(ps[0:GT, 0, 0:G], trel[0:G, :], ident[0:G, 0:G]).then_inc(s_tminps, 1)
            for j, a in enumerate((GMIN, GW, GV)):
                last = nc.tensor.matmul(ps_flat[0:1, 1024 + j * P:1024 + j * P + G], gm[0:G, a:a + 1], ident[0:G, 0:G],
                                        start=True, stop=True)
            last.then_inc(s_rowps, 1)
            pe.wait_ge(s_tminT, 1)
            pe.wait_ge(s_rep, 2)
            nc.tensor.matmul(ps[:, 1, 0:G], rep[:, :], tminT[:, 0:G], start=True, stop=True).then_inc(s_tminps, 1)
            pe.wait_ge(s_rows, 3)
            pe.wait_ge(s_keyT, 2)
            pe.wait_ge(s_w, 64)

            def turn_sums(l):
                def turn(c, first=False):
                    pe.wait_ge(s_accC[l], c + 1)
                    if not first:
                        pe.wait_ge(s_outev[l], c)
                    for t in range(CH):
                        last = nc.tensor.transpose(ps_out[:, t // 5, t % 5, 0:D1], accC[:, t, :], ident[0:D1, 0:D1])
                    last.then_inc(s_outps[l], 1)

                turn(0, first=True)
                with pe.Fori(1, NCH) as c:
                    turn(c)

            def self_chunk(c, first=False):
                pe.wait_ge(s_hc, c + 1)
                for j in range(CP):
                    last = nc.tensor.transpose(ps_hT[:, j * P:(j + 1) * P],
                                               hc[:, 2 * j:2 * j + 2, :].rearrange("p t f -> p (t f)"), ident[:, :])
                last.then_inc(s_hTps, 1)
                pe.wait_ge(s_hT, c + 1)
                if not first:
                    pe.wait_ge(s_self, c)
                for j in range(CP):
                    for half in range(2):
                        part = slice(half * D, (half + 1) * D)
                        last = nc.tensor.matmul(ps_self[:, half, j * D:(j + 1) * D], hT[part, j, :], selfW[part, :],
                                                start=True, stop=True)
                last.then_inc(s_selfps, 1)

            for l in range(2):
                if l == 1:
                    turn_sums(0)
                    self_chunk(0, first=True)
                    with pe.Fori(1, NCH) as c:
                        self_chunk(c)
                    pe.wait_ge(s_outev[0], NCH)
                    pe.wait_ge(s_self, NCH)

                def sum_group(g, b, gathers):
                    wins, spans = group_counts(pe, g)
                    with pe.Fori(0, wins):
                        pe.wait_ge(s_gath[l][b], gathers)
                        k = pe_wins.value()
                        for c in range(GT):
                            u, i = divmod(c, BANKT)
                            if i == 0:
                                pe.wait_ge(s_agg[l], k * UNITS + (u + 1))
                            if c % (GT // HB) == 0:
                                pe.wait_ge(s_hot[l], k * HB + (c // (GT // HB) + 1))
                            for half in range(HALVES[l]):
                                last = nc.tensor.matmul(ps[half * D:half * D + M[l], u, i * COLS:(i + 1) * COLS],
                                                        gath[:, b, c, 0:M[l]],
                                                        hot_v[l][:, c, half * COLS:(half + 1) * COLS],
                                                        start=True, stop=True)
                            if i == BANKT - 1:
                                last.then_inc(s_tiles[l], 1)
                        pe.wait_ge(s_agg[l], k * UNITS + 2 * UNITS)
                        pe.wait_ge(s_y[l], k + 1)
                        for r in range(RC):
                            last = nc.tensor.matmul(ps_y[l], agg[0:MP[l], r, :, :].rearrange("i c n -> i (c n)"),
                                                    W[l][:, r, :], start=(r == 0), stop=(r == RC - 1))
                        last.then_inc(s_yps[l], 1)
                        with pe.Fori(0, spans):
                            a = pe_spans.value()
                            pe.wait_ge(s_y[l], k + 2)
                            pe.wait_ge(s_slothot[l], a + 1)
                            nc.tensor.matmul(ps_acc[l], y[:, 0:M[l]], slothot[:, :], start=True, stop=True)\
                                .then_inc(s_span[l], 1)
                            pe_spans.add(1)
                        pe_wins.add(1)
                    pe.wait_ge(s_span[l], pe_spans.value())
                    pe.sem_inc(s_group[l], 1)

                pe_wins.zero()
                pe_spans.zero()
                with pe.Fori(0, G // 2 - 1) as i:
                    for b in range(2):
                        sum_group(i * 2 + b, b, (i + 1) * (16 * GT))
                sum_group(G - 2, 0, 16 * GT * (G // 2))
                sum_group(G - 1, 1, 16 * (GT * (G // 2 - 1) + LASTT))
            turn_sums(1)

        @block.vector
        def _(dve):
            for a in range(4):
                nc.vector.memset(nat_i[a][96:G, LASTE:GE], NO_EDGE if a in (T16, T32) else 0).then_inc(s_pad, 1)
            nc.vector.memset(xs[96:P, :, :], 0.0).then_inc(s_xzero, 1)
            nc.vector.memset(W[0][:, :, :], 0.0).then_inc(s_wzero, 1)
            dve.wait_ge(s_wzero, 1)
            nc.vector.memset(W[0][D:D1, :, D:D1], 1.0).then_inc(s_wzero, 1)
            for l in range(2):
                nc.vector.memset(keyT[l][:, G:G + 1, :], -1.0).then_inc(s_keypad, 1)

            dve_wins = Count(dve, "dve_wins", MAXW * G)
            dve_spans = Count(dve, "dve_spans", MAXW * MAXV * G)

            def wide(v):
                return v[:, :].rearrange("p (t a) -> p t a", a=1).broadcast_to([P, CH, D])

            def ln_stats(l, c):
                ch = Chain(dve, s_ln[l], c * 6)
                hh = chunk(h, c)
                ch.step(nc.vector.tensor_reduce(out=mean[:, :], in_=chunk(xs, c), axis=AX.X, op=ALU.add))
                ch.step(nc.vector.tensor_scalar(mean[:, :], mean[:, :], 1.0 / D, None, ALU.mult))
                ch.step(nc.vector.tensor_tensor(hh, chunk(xs, c), wide(mean), ALU.subtract))
                ch.step(nc.vector.tensor_tensor(sq[:, :, :], hh, hh, ALU.mult))
                ch.step(nc.vector.tensor_reduce(out=var[:, :], in_=sq[:, :, :], axis=AX.X, op=ALU.add))
                nc.vector.tensor_scalar(var[:, :], var[:, :], 1.0 / D, EPS, ALU.mult, ALU.add)\
                    .then_inc(s_var[l], 1)

            def ln_scale(l, c):
                ch = Chain(dve, s_ln[l], c * 6 + 5)
                dve.wait_ge(s_std[l], c + 1)
                ch.step(nc.vector.reciprocal(rstd[:, :], std[:, :]))
                nc.vector.scalar_tensor_tensor(chunk(h, c), chunk(h, c), 0.0, wide(rstd), ALU.max, ALU.mult)\
                    .then_inc(s_h[l], 1)

            dve.wait_ge(s_xzero, 1)
            dve.wait_ge(s_x, 48)
            ln_stats(0, 0)
            with dve.Fori(0, NCH - 1) as c:
                ln_scale(0, c)
                ln_stats(0, c + 1)
            ln_scale(0, NCH - 1)

            dve.wait_ge(s_cops, 1)
            nc.vector.tensor_copy(coT[:, :], ps[0:NB, 4, 0:R[1]]).then_inc(s_coT, 1)

            def tiles(t):
                return t.rearrange("g (c p) -> g c p", p=P)

            setup = Chain(dve, s_setup)
            dve.wait_ge(s_edges, 16 * 10)
            setup.step(nc.vector.tensor_copy(nat[DST], nat_i[DST]))
            setup.step(nc.vector.tensor_reduce(out=tmin[0:G, :], in_=tiles(nat[DST]), axis=AX.X, op=ALU.min))
            setup.step(nc.vector.tensor_reduce(out=tmax[0:G, :], in_=tiles(nat[DST]), axis=AX.X, op=ALU.max))
            setup.step(nc.vector.tensor_tensor(tiles(nat[DST]), tiles(nat[DST]),
                                               tmin[0:G, :].rearrange("g (c a) -> g c a", a=1).broadcast_to([G, GT, P]),
                                               ALU.subtract))
            for l, a in enumerate((T16, T32)):
                nc.vector.scalar_tensor_tensor(nat[a], nat[DST], float(R[l]), nat_i[a], ALU.mult, ALU.add)\
                    .then_inc(s_keys, 1)
            dve.wait_ge(s_w1ps, 1)
            nc.vector.tensor_copy(W[1][:, :, :], ps_flat[:, 2048:2048 + D * RC].rearrange("i (o r) -> i r o", r=RC))\
                .then_inc(s_w1, 1)
            setup.step(nc.vector.tensor_reduce(out=gm[0:G, GMIN:GMIN + 1], in_=tmin[0:G, :], axis=AX.X, op=ALU.min))
            setup.step(nc.vector.tensor_reduce(out=gm[0:G, GMAX:GMAX + 1], in_=tmax[0:G, :], axis=AX.X, op=ALU.max))
            setup.step(nc.vector.tensor_tensor(tmax[0:G, :], tmax[0:G, :], tmin[0:G, :], ALU.subtract))
            setup.step(nc.vector.tensor_scalar(trel[0:G, :], tmin[0:G, :], gm[0:G, GMIN:GMIN + 1], None, ALU.subtract))
            setup.step(nc.vector.tensor_reduce(out=gi[0:G, 0:1], in_=tmax[0:G, :], axis=AX.X, op=ALU.max))
            setup.step(nc.vector.tensor_tensor(gi[0:G, 1:2], gm[0:G, GMAX:GMAX + 1], gm[0:G, GMIN:GMIN + 1],
                                               ALU.subtract))
            for j, n in enumerate((NW, SPAN)):
                setup.step(nc.vector.tensor_scalar(gj[0:G, j:j + 1], gi[0:G, j:j + 1], n.bit_length() - 1, None,
                                                   ALU.arith_shift_right))
            nc.vector.tensor_scalar(gm[0:G, GW:GV + 1], gj[0:G, :], 1.0, None, ALU.add).then_inc(s_gm, 1)
            dve.wait_ge(s_lane, 1)
            setup.step(nc.vector.tensor_scalar(lane8i[:, :], lane[:, :], NW - 1, None, ALU.bitwise_and))
            setup.step(nc.vector.tensor_copy(lane8[:, :], lane8i[:, :]))
            for l, bank in enumerate((0, 4)):
                dve.wait_ge(s_keyps, l + 1)
                nc.vector.tensor_copy(keyT[l][:, 0:G, :], ps_flat[:, bank * 512:bank * 512 + GT * P]
                                      .rearrange("p (c g) -> p g c", c=GT)[:, 0:G, :]).then_inc(s_keyT, 1)
            dve.wait_ge(s_tminps, 1)
            nc.vector.tensor_copy(tminT[:, 0:G], ps[0:GT, 0, 0:G]).then_inc(s_tminT, 1)
            dve.wait_ge(s_rowps, 1)
            nc.vector.tensor_copy(rowf[:, :, 0:G], ps_flat[0:1, 1024:1024 + 3 * P]
                                  .rearrange("p (a g) -> p a g", a=3)[:, :, 0:G]).then_inc(s_rowf, 1)
            dve.wait_ge(s_rowf, 1)
            nc.vector.tensor_copy(rows[:, BASE, 0:G], rowf[:, BASE, 0:G]).then_inc(s_rows, 1)
            nc.vector.scalar_tensor_tensor(rows[:, COUNTS, 0:G], rowf[:, WINS, 0:G], float(1 << VBITS),
                                           rowf[:, SPANS, 0:G], ALU.mult, ALU.add).then_inc(s_rows, 1)
            dve.wait_ge(s_tminps, 2)
            nc.vector.tensor_scalar(slot[:, :], ps[:, 1, 0:G], lane8[:, :], None, ALU.add).then_inc(s_rows, 1)

            for l in range(2):
                if l == 1:
                    with dve.Fori(0, NCH) as c:
                        x4 = chunk(xs, c).rearrange("p (b t) f -> p b t f", b=2)
                        dve.wait_ge(s_outps[0], c + 1)
                        nc.vector.tensor_tensor(x4, x4, ps_out[:, :, :, 0:D], ALU.add).then_inc(s_xsum, 1)
                        nc.vector.tensor_scalar(rdeg[:, bass.ds(c * CH, CH)]
                                                .rearrange("p (b t a) -> p b t a", b=2, a=1),
                                                ps_out[:, :, :, D:D1], 1.0, None, ALU.max).then_inc(s_outev[0], 1)
                    dve.wait_ge(s_xsum, NCH)
                    dve.wait_ge(s_store[0], 16 * NCH)

                    def add_self(c):
                        dve.wait_ge(s_selfps, c + 1)
                        by_half = chunk(xs, c).rearrange("p (j a) f -> p a j f", a=2)
                        nc.vector.tensor_tensor(by_half, by_half, ps_self.rearrange("p a (j f) -> p a j f", f=D),
                                                ALU.add).then_inc(s_self, 1)

                    ln_stats(1, 0)
                    with dve.Fori(0, NCH - 1) as c:
                        ln_scale(1, c)
                        ln_stats(1, c + 1)
                        add_self(c)
                    ln_scale(1, NCH - 1)
                    add_self(NCH - 1)
                    dve.wait_ge(s_self, NCH)
                    dve.wait_ge(s_w, 64)
                    nc.vector.tensor_tensor(xs[:, :, :], xs[:, :, :], biasB[:, :, :].broadcast_to([P, TT, D]), ALU.add)\
                        .then_inc(s_base, 1)
                    dve.wait_ge(s_outev[0], NCH)
                    nc.vector.reciprocal(rdeg[:, :], rdeg[:, :]).then_inc(s_base, 1)
                if l == 1:
                    dve.wait_ge(s_accC[0], NCH)
                nc.vector.memset(accT[:, :], 0.0).then_inc(s_acc[l], 1)
                nc.vector.memset(slotw[:, :], 0.0).then_inc(s_slotw[l], 1)
                nc.vector.memset(slotv[:, :], 0.0).then_inc(s_spanstep[l], 1)
                nc.vector.memset(y[:, :], 0.0).then_inc(s_y[l], 1)
                dve.wait_ge(s_const, 4)
                dve.wait_ge(s_rows, 3)
                dve.wait_ge(s_keyT, 2)
                dve.wait_ge(s_keypad, 2)
                dve.wait_ge(s_srcT, 1)
                dve_wins.zero()
                dve_spans.zero()

                def build_onehot():
                    HC = GT // HB
                    for i in range(HB):
                        nc.vector.tensor_tensor(
                            hot_v[l][:, i * HC:(i + 1) * HC, :],
                            iotaK[l][:, :, :, :].rearrange("p (a h) r n -> p a (h r n)", a=1)
                            .broadcast_to([P, HC, KEYS[l]]),
                            keyw[:, i * HC:(i + 1) * HC].rearrange("p (c a) -> p c a", a=1)
                            .broadcast_to([P, HC, KEYS[l]]), ALU.is_equal).then_inc(s_hot[l], 1)

                nc.vector.tensor_copy(keyw[:, :], keyT[l][:, 0, :]).then_inc(s_keyw[l], 1)
                dve.wait_ge(s_keyw[l], 1)
                build_onehot()

                with dve.Fori(0, G) as g:
                    wins, spans = group_counts(dve, g)
                    base = dve.value_load(rows[0:1, BASE, bass.ds(g, 1)], min_val=0, max_val=N - 1)
                    dve.wait_ge(s_slotw[l], dve_wins.value() + g + 1)
                    nc.vector.tensor_copy(slotw[:, :], slot[:, bass.ds(g, 1)]).then_inc(s_slotw[l], 1)
                    with dve.Fori(0, wins) as w:
                        k = dve_wins.value()
                        dve.wait_ge(s_slotw[l], k + g + 2)
                        dve.wait_ge(s_spanstep[l], dve_spans.value() + 1)
                        nc.vector.tensor_copy(slotv[:, :], slotw[:, :]).then_inc(s_slotv[l], 1)
                        dve.wait_ge(s_slotv[l], k + 1)
                        nc.vector.tensor_scalar(slotw[:, :], slotw[:, :], float(NW), None, ALU.add)\
                            .then_inc(s_slotw[l], 1)
                        dve.wait_ge(s_hot[l], k * HB + HB)
                        with dve.If(w + 1 < wins):
                            nc.vector.tensor_scalar(keyw[:, :], keyw[:, :], float(-KEYS[l]), None, ALU.add)\
                                .then_inc(s_keyw[l], 1)
                        with dve.Else():
                            nc.vector.tensor_copy(keyw[:, :], keyT[l][:, bass.ds(g + 1, 1), :]
                                                  .rearrange("p a c -> p (a c)")).then_inc(s_keyw[l], 1)
                        dve.wait_ge(s_keyw[l], k + 2)
                        dve.wait_ge(s_tiles[l], k * UNITS + UNITS)
                        build_onehot()
                        dve.wait_ge(s_yps[l], k + 1)
                        nc.vector.tensor_copy(y[:, 0:M[l]], ps_y[l]).then_inc(s_y[l], 1)
                        with dve.Fori(0, spans) as v:
                            a = dve_spans.value()
                            dve.wait_ge(s_spanstep[l], a + 1)
                            nc.vector.tensor_scalar(slothot[:, :], iotaS[:, :], slotv[:, :], None, ALU.is_equal)\
                                .then_inc(s_slothot[l], 1)
                            dve.wait_ge(s_slothot[l], a + 1)
                            nc.vector.tensor_scalar(slotv[:, :], slotv[:, :], float(-SPAN), None, ALU.add)\
                                .then_inc(s_spanstep[l], 1)
                            dve.wait_ge(s_span[l], a + 1)
                            dve.wait_ge(s_acc[l], a + 1)
                            start = nc.s_assert_within(
                                base + v * SPAN, 0, N - 1,
                                skip_runtime_bounds_check_because="it is at most the group's largest receiver")
                            win = accT[0:M[l], bass.ds(start, SPAN)]
                            nc.vector.tensor_tensor(win, win, ps_acc[l], ALU.add).then_inc(s_acc[l], 1)
                            dve_spans.add(1)
                        dve_wins.add(1)

            dve.wait_ge(s_base, 2)
            dve.wait_ge(s_store[1], 16 * NCH)
            with dve.Fori(0, NCH) as c:
                dve.wait_ge(s_outps[1], c + 1)
                nc.vector.tensor_tensor(chunk(h, c).rearrange("p (b t) f -> p b t f", b=2), ps_out[:, :, :, 0:D],
                                        rdeg[:, bass.ds(c * CH, CH)].rearrange("p (b t a) -> p b t a", b=2, a=1)
                                        .broadcast_to([P, 2, 5, D]), ALU.mult).then_inc(s_outev[1], 1)
                dve.wait_ge(s_outev[1], c + 1)
                nc.vector.tensor_tensor(chunk(h, c), chunk(h, c), chunk(xs, c), ALU.add).then_inc(s_final, 1)


_INS = ["x", "src", "dst", "edge_type_16", "edge_type_32", "L0_gnn_weight", "L1_gnn_basis", "L1_gnn_coeff",
        "L1_gnn_self_weight", "L1_gnn_bias"]


def kernel(**inputs):
    import numpy as np
    import concourse.bacc as bacc
    from concourse import mybir as mb
    from concourse.bass_utils import run_bass_kernel_spmd

    nc = bacc.Bacc("TRN2", target_bir_lowering=False, num_devices=1)
    arrays, args = {}, []
    for name in _INS:
        a = np.ascontiguousarray(inputs[name])
        arrays[f"in_{name}"] = a
        args.append(nc.dram_tensor(f"in_{name}", a.shape, mb.dt.from_np(a.dtype), kind="ExternalInput").ap())
    shape = arrays["in_x"].shape
    args.append(nc.dram_tensor("out_x", shape, mb.dt.float32, kind="ExternalOutput").ap())
    two_layer_gnn_kernel(nc, *args)
    r = run_bass_kernel_spmd(nc, [arrays], core_ids=[0])
    return r.results[0]["out_x"]
```

```python
import concourse.bass as bass
from concourse import mybir
from contextlib import ExitStack


def two_layer_gnn_kernel(nc, x, src, dst, type16, type32, weight0, basis, coeff, self_weight, bias, out):
    f32, i32, bf16 = mybir.dt.float32, mybir.dt.int32, mybir.dt.bfloat16
    ALU, ACT, AX = mybir.AluOpType, mybir.ActivationFunctionType, mybir.AxisListType

    N, D = x.shape
    E = src.shape[0]
    R = (weight0.shape[0], coeff.shape[0])
    NB = basis.shape[0]
    P = 128
    D1 = D + 1
    TT = 50
    NP = N // TT
    assert NP * TT == N and NP <= P
    CH = 10
    NCH = TT // CH
    CP = CH // 2
    GT = 16
    GE = GT * P
    G = -(-E // GE)
    assert G % 2 == 0
    LASTE = E - (G - 1) * GE
    LASTT = -(-LASTE // P)
    REST = -LASTE % P
    NW = P // GT
    KEYS = [NW * R[l] for l in range(2)]
    COLS = 128
    HALVES = [KEYS[l] // COLS for l in range(2)]
    RC = COLS // NW
    M = [D1, D]
    MP = [D1, 2 * D]
    assert HALVES == [1, 2]
    BANKT = 4
    UNITS = GT // BANKT
    PICKS = 2
    SPAN = P
    MAXW = (N - 1) // NW + 1
    MAXV = (N - 1) // SPAN + 1
    VBITS = MAXV.bit_length()
    ROW = 80
    NO_EDGE = -1000000
    EPS = 1e-5

    table = [nc.dram_tensor(f"table{l}", (P * TT, D), f32, kind="Internal").ap() for l in range(2)]
    table_v = [table[l].rearrange("(p t) f -> p (t f)", p=P) for l in range(2)]
    x_v = x.rearrange("(p t) f -> p (t f)", t=TT)
    out_v = out.rearrange("(p t) f -> p (t f)", t=TT)

    ctx = ExitStack()
    with ctx:
        def sb(name, shape, dt=f32):
            return ctx.enter_context(nc.sbuf_tensor(name, shape, dt))

        def sem(name):
            return ctx.enter_context(nc.semaphore(name))

        def sems(name):
            return [sem(f"{name}{l}") for l in range(2)]

        xs = sb("xs", [P, TT, D])
        h = sb("h", [P, TT, D])
        h3 = sb("h3", [P, TT, 3, D], bf16)
        scratch = sb("scratch", [P, max(D * D, TT * D)])
        bas = scratch[0:NB, 0:D * D]
        hT = scratch[:, 0:TT * D].rearrange("p (j n) -> p j n", n=P)
        rest = scratch[:, 0:TT * D].rearrange("p (t f) -> p t f", f=D)
        sends = scratch[:, :].bitcast(bf16)[:, 0:TT * P].rearrange("p (t e) -> p t e", e=P)
        srcB = sb("srcB", [P, P], i32)
        offset = sb("offset", [P, P], bf16)
        first = sb("first", [P, 1])
        iotaT = sb("iotaT", [P, TT, 8], bf16)
        accT = sb("accT", [D1, P * TT])
        W = [sb("W0", [D1, R[0], D1]), sb("W1", [P, RC, D])]
        selfW = sb("selfW", [P, P])
        biasB = sb("biasB", [P, 1, D])
        srcT = sb("srcT", [P, G, GT])
        keyT = [sb(f"keyT{l}", [P, G + 1, GT]) for l in range(2)]
        gath = sb("gath", [P, 2, GT, ROW])
        idx = sb("idx", [P, 2, GT], i32)
        onehot = sb("onehot", [P, 2, 2048])
        agg = sb("agg", [P, RC, GT, NW])
        natx = sb("natx", [P, 2048])
        keyw = sb("keyw", [P, GT])
        iotaK = [sb(f"iotaK{l}", [P, HALVES[l], RC, NW]) for l in range(2)]
        iotaS = sb("iotaS", [P, SPAN])
        slot = sb("slot", [P, G])
        slotw = sb("slotw", [P, 1])
        slotv = sb("slotv", [P, 1])
        slothot = sb("slothot", [P, SPAN])
        y = sb("y", [P, D1])
        ident = sb("ident", [P, P])
        rep = sb("rep", [GT, P])
        rowf = sb("rowf", [1, 3, P])
        rows = sb("rows", [1, 3, P], i32)
        BASE, WINS, SPANS = range(3)
        COUNTS = 1
        tmin = sb("tmin", [P, GT])
        tmax = sb("tmax", [P, GT])
        trel = sb("trel", [P, GT])
        tminT = sb("tminT", [GT, P])
        gm = sb("gm", [P, 8])
        GMIN, GMAX, GW, GV = range(4)
        gi = sb("gi", [P, 2], i32)
        gj = sb("gj", [P, 2], i32)
        lane = sb("lane", [P, 1], i32)
        lane8i = sb("lane8i", [P, 1], i32)
        lane8 = sb("lane8", [P, 1])
        coT = sb("coT", [NB, R[1]])
        co = sb("co", [R[1], NB])
        sums = sb("sums", [P, CH])
        var = sb("var", [P, CH])
        std = sb("std", [P, CH])
        rstd = sb("rstd", [P, CH])
        eps = sb("eps", [P, 1])
        sq = sb("sq", [P, CH, D])
        rdeg = sb("rdeg", [P, TT])

        nat = [onehot[0:G, 0, :], agg[0:G, :, :, :].rearrange("p r c n -> p (r c n)"), onehot[0:G, 1, :],
               natx[0:G, :]]
        nat_i = [t.bitcast(i32) for t in nat]
        SRC, DST, T16, T32 = range(4)
        hot_v = [onehot[:, :, :].rearrange("p a n -> p (a n)")[:, 0:GT * KEYS[l]]
                 .rearrange("p (c k) -> p c k", c=GT) for l in range(2)]

        ps = ctx.enter_context(nc.psum_tensor("ps", [P, 8, 512], f32))
        ps_flat = ps[:, :, :].rearrange("p b n -> p (b n)")
        ps_y = [ps[:, 4, 0:M[l]] for l in range(2)]
        ps_acc = [ps[0:M[l], 5, 0:SPAN] for l in range(2)]
        ps_out = [ps[:, 2 * i:2 * i + 2, 0:480].rearrange("p b (t n) -> p b t n", n=96) for i in range(2)]
        ps_hT = [ps_flat[:, (4 + 2 * i) * 512:(4 + 2 * i) * 512 + CP * P] for i in range(2)]
        ps_self = ps_flat[:, 0:TT * D]
        ps_pick = ps[:, 6, 0:3 * D]
        ps_rel = ps[0:GT, 6, 0:G]
        ps_slot = ps[:, 6, P:P + G]
        ps_rows = ps[0:1, 7, 0:3 * P]

        accT_t = accT[:, :].rearrange("d (p t) -> d t p", t=TT)

        s_pad = sem("s_pad")
        s_xzero = [sem("s_xzero_first"), sem("s_xzero_rest")]
        s_x = [sem("s_x_first"), sem("s_x_rest")]
        s_src = sem("s_src")
        s_edges = sem("s_edges")
        s_wzero = sem("s_wzero")
        s_w = sem("s_w")
        s_basis = sem("s_basis")
        s_id0 = sem("s_id0")
        s_ident = sem("s_ident")
        s_rep = sem("s_rep")
        s_lane = sem("s_lane")
        s_const = sem("s_const")
        s_issue = sem("s_issue")
        s_srcf = sem("s_srcf")
        s_srcps = sem("s_srcps")
        s_srcT = sem("s_srcT")
        s_setup = sem("s_setup")
        s_keys = sem("s_keys")
        s_keyps = sem("s_keyps")
        s_keyT = sem("s_keyT")
        s_gm = sem("s_gm")
        s_tminps = sem("s_tminps")
        s_tminT = sem("s_tminT")
        s_rowps = sem("s_rowps")
        s_rows = sem("s_rows")
        s_cops = sem("s_cops")
        s_coT = sem("s_coT")
        s_w1ps = sem("s_w1ps")
        s_w1 = sem("s_w1")
        s_eps = sem("s_eps")
        s_table = sem("s_table")
        s_ln, s_centered, s_sq = sems("s_ln"), sems("s_centered"), sems("s_sq")
        s_var, s_std, s_h = sems("s_var"), sems("s_std"), sems("s_h")
        s_store = sems("s_store")
        s_hTps, s_hT, s_selfps, s_self = [sem(n) for n in ("s_hTps", "s_hT", "s_selfps", "s_self")]
        s_idx = sems("s_idx")
        s_gath = [[[sem(f"s_gath{l}{b}{u}") for u in range(UNITS)] for b in range(2)] for l in range(2)]
        s_group = sems("s_group")
        s_hi, s_rest, s_mid, s_lo = sems("s_hi"), sems("s_rest"), sems("s_mid"), sems("s_lo")
        s_srcB, s_offset, s_sends = sems("s_srcB"), sems("s_offset"), sems("s_sends")
        s_pickps, s_picked = sems("s_pickps"), sems("s_picked")
        s_keyw = sems("s_keyw")
        s_hot = sems("s_hot")
        s_tiles = sems("s_tiles")
        s_agg = sems("s_agg")
        s_yps = sems("s_yps")
        s_y = sems("s_y")
        s_slotw = sems("s_slotw")
        s_slotv = sems("s_slotv")
        s_slothot = sems("s_slothot")
        s_spanstep = sems("s_spanstep")
        s_span = sems("s_span")
        s_acc = sems("s_acc")
        s_keypad = sem("s_keypad")
        s_rowf = sem("s_rowf")
        s_zeroed, s_outps, s_outev = sems("s_zeroed"), sems("s_outps"), sems("s_outev")
        s_xsum = sem("s_xsum")
        s_base = sem("s_base")
        s_final = sem("s_final")
        s_out = sem("s_out")

        class Chain:

            def __init__(self, eng, s):
                self.eng, self.s, self.n = eng, s, 0

            def step(self, ins):
                self.n += 1
                ins.then_inc(self.s, 1)
                self.eng.wait_ge(self.s, self.n)

        def chunk(t, c):
            return t[:, c * CH:(c + 1) * CH, :]

        class Count:

            def __init__(self, eng, name, high):
                self.eng, self.reg, self.high = eng, eng.alloc_register(name), high

            def zero(self):
                self.eng.reg_mov(self.reg, 0)

            def add(self, n):
                self.eng.reg_add(self.reg, self.reg, n)

            def value(self):
                return self.eng.snap(self.reg, min_val=0, max_val=self.high)

        def group_counts(eng, g):
            both = eng.value_load(rows[0:1, COUNTS, bass.ds(g, 1)], min_val=0, max_val=MAXW << VBITS | MAXV)
            wins = eng.snap(both >> VBITS, min_val=1, max_val=MAXW)
            spans = eng.snap(both & ((1 << VBITS) - 1), min_val=1, max_val=MAXV)
            return wins, spans

        def gathers(l, g, b, u):
            if b == 0 and u == UNITS - 1:
                return (g >> 1) * (16 * (BANKT - PICKS)) + 16 * BANKT
            if isinstance(g, int) and g == G - 1:
                return 16 * (BANKT * (G // 2 - 1) + min(max(LASTT - u * BANKT, 0), BANKT))
            return ((g - b) >> 1) * (16 * BANKT) + 16 * BANKT

        block = ctx.enter_context(nc.Block())

        @block.sync
        def _(sp):
            for i, (t0, t1) in enumerate(((0, CH), (CH, TT))):
                for p0, p1 in ((0, 96), (96, 112), (112, NP)):
                    if p0 == 96:
                        sp.wait_ge(s_xzero[i], 1)
                    sp.dma_start(xs[p0:p1, t0:t1, :].rearrange("p t f -> p (t f)"), x_v[p0:p1, t0 * D:t1 * D])\
                      .then_inc(s_x[i], 16)
            sp.wait_ge(s_pad, 1)
            sp.dma_start(nat_i[SRC][0:96, :], src[0:96 * GE].rearrange("(g e) -> g e", e=GE)).then_inc(s_src, 16)
            sp.dma_start(nat_i[SRC][96:G - 1, :], src[96 * GE:(G - 1) * GE].rearrange("(g e) -> g e", e=GE))\
              .then_inc(s_src, 16)
            sp.dma_start(nat_i[SRC][G - 1:G, 0:LASTE], src[(G - 1) * GE:E].rearrange("(g e) -> g e", g=1))\
              .then_inc(s_src, 16)
            sp.dma_start(bas, basis.rearrange("b i o -> b (i o)")).then_inc(s_basis, 16)
            sp.dma_start(co[:, :], coeff).then_inc(s_basis, 16)
            sp.wait_ge(s_pad, 4)
            for a, arr in ((DST, dst), (T16, type16), (T32, type32)):
                t = nat_i[a]
                sp.dma_start(t[0:96, :], arr[0:96 * GE].rearrange("(g e) -> g e", e=GE)).then_inc(s_edges, 16)
                sp.dma_start(t[96:G - 1, :], arr[96 * GE:(G - 1) * GE].rearrange("(g e) -> g e", e=GE))\
                  .then_inc(s_edges, 16)
                sp.dma_start(t[G - 1:G, 0:LASTE], arr[(G - 1) * GE:E].rearrange("(g e) -> g e", g=1))\
                  .then_inc(s_edges, 16)

            for e0, e1 in ((LASTE, LASTE + REST), (LASTE + REST, GE)):
                if e1 > e0:
                    sp.dma_start(nat_i[DST][G - 1:G, e0:e1], dst[E - (e1 - e0):E].rearrange("(g e) -> g e", g=1))\
                      .then_inc(s_edges, 16)

            sp.wait_ge(s_wzero, 3)
            sp.dma_start(W[0][0:D, :, 0:D], weight0.rearrange("r i o -> i r o")).then_inc(s_w, 16)
            for half in range(2):
                part = slice(half * D, (half + 1) * D)
                sp.dma_start(selfW[part, part], self_weight).then_inc(s_w, 16)
            sp.dma_start(biasB[:, 0, :], bias.rearrange("(a n) -> a n", a=1).broadcast_to([P, D]))\
              .then_inc(s_w, 16)

            for l in range(2):
                for c in range(NCH):
                    sp.wait_ge(s_h[l], c + 1)
                    sp.dma_start(table_v[l][:, c * (CH * D):(c + 1) * (CH * D)],
                                 chunk(h, c).rearrange("p t f -> p (t f)")).then_inc(s_store[l], 16)

                with sp.Fori(0, G // 2 - 1) as i:
                    for b in range(2):
                        sp.wait_ge(s_offset[l], i * PICKS + (b + 1))
                        sp.dma_start(srcB[:, :], src[bass.ds(i * (2 * GE) + (2 * GE + (GT - PICKS + b) * P), P)]
                                     .rearrange("(a e) -> a e", a=1).broadcast_to([P, P])).then_inc(s_srcB[l], 16)

            for c in range(NCH):
                sp.wait_ge(s_final, c + 1)
                for p0, p1 in ((0, 112), (112, NP)):
                    sp.dma_start(out_v[p0:p1, c * (CH * D):(c + 1) * (CH * D)],
                                 h[p0:p1, c * CH:(c + 1) * CH, :].rearrange("p t f -> p (t f)"))\
                      .then_inc(s_out, 16)
            sp.wait_ge(s_out, 32 * NCH)

        @block.gpsimd
        def _(pool):
            nc.gpsimd.memset(xs[96:P, CH:TT, :], 0.0).then_inc(s_xzero[1], 1)
            pool.wait_ge(s_xzero[1], 1)
            nc.gpsimd.memset(W[0][:, :, :], 0.0).then_inc(s_wzero, 1)
            nc.gpsimd.memset(selfW[:, :], 0.0).then_inc(s_wzero, 1)
            nc.gpsimd.memset(ident[:, :], 0.0).then_inc(s_id0, 1)
            nc.gpsimd.memset(rep[:, :], 1.0).then_inc(s_id0, 1)
            pool.wait_ge(s_id0, 2)
            nc.gpsimd.affine_select(out=ident[:, :], in_=ident[:, :], compare_op=ALU.not_equal, fill=1.0, base=0,
                                    pattern=[[-1, P]], channel_multiplier=1).then_inc(s_ident, 1)
            nc.gpsimd.affine_select(out=rep[:, :], in_=rep[:, :], compare_op=ALU.is_ge, fill=0.0, base=0,
                                    pattern=[[1, P]], channel_multiplier=-NW).then_inc(s_rep, 1)
            pool.wait_ge(s_rep, 1)
            nc.gpsimd.affine_select(out=rep[:, :], in_=rep[:, :], compare_op=ALU.is_ge, fill=0.0, base=NW - 1,
                                    pattern=[[-1, P]], channel_multiplier=NW).then_inc(s_rep, 1)
            nc.gpsimd.iota(lane[:, :], [[0, 1]], base=0, channel_multiplier=1).then_inc(s_lane, 1)
            for l in range(2):
                nc.gpsimd.iota(iotaK[l][:, :, :, :], [[RC, HALVES[l]], [1, RC], [R[l], NW]], base=0,
                               channel_multiplier=0, allow_small_or_imprecise_dtypes=True).then_inc(s_const, 1)
            nc.gpsimd.iota(iotaS[:, :], [[1, SPAN]], base=0, channel_multiplier=0,
                           allow_small_or_imprecise_dtypes=True).then_inc(s_const, 1)
            nc.gpsimd.iota(iotaT[:, :, :], [[1, TT], [0, 8]], base=0, channel_multiplier=0,
                           allow_small_or_imprecise_dtypes=True).then_inc(s_const, 1)
            nc.gpsimd.iota(first[:, :], [[0, 1]], base=0, channel_multiplier=-TT,
                           allow_small_or_imprecise_dtypes=True).then_inc(s_const, 1)
            nc.gpsimd.memset(gath[:, :, :, :], 1.0).then_inc(s_const, 1)
            pool.wait_ge(s_const, 6)
            nc.gpsimd.memset(accT[:, :], 0.0).then_inc(s_zeroed[0], 1)

            for l in range(2):
                if l == 1:
                    for c in range(NCH):
                        pool.wait_ge(s_outps[0], c + 1)
                        nc.gpsimd.memset(accT_t[:, c * CH:(c + 1) * CH, :], 0.0).then_inc(s_zeroed[1], 1)

                def gather_group(b, tiles):
                    for c in range(tiles):
                        nc.gpsimd.indirect_dma_start(
                            out=gath[:, b, c, 0:D], out_offset=None, in_=table[l],
                            in_offset=bass.IndirectOffsetOnAxis(ap=idx[:, b, c:c + 1], axis=0))\
                            .then_inc(s_gath[l][b][c // BANKT], 16)

                pool.wait_ge(s_store[l], 16 * NCH)
                for b in range(2):
                    pool.wait_ge(s_idx[l], b + 1)
                    gather_group(b, GT)

                def gather_again(g, b, tiles):
                    pool.wait_ge(s_group[l], g - 1)
                    pool.wait_ge(s_idx[l], g + 1)
                    pool.sem_inc(s_issue, 1)
                    gather_group(b, tiles)

                with pool.Fori(1, G // 2 - 1) as i:
                    for b in range(2):
                        gather_again(i * 2 + b, b, GT - PICKS if b == 0 else GT)
                gather_again(G - 2, 0, GT - PICKS)
                gather_again(G - 1, 1, LASTT)

        @block.scalar
        def _(act):
            act_wins = Count(act, "act_wins", MAXW * G)

            act.wait_ge(s_eps, 1)
            nc.scalar.activation(std[:, 0:1], eps[:, :], ACT.Sqrt).then_inc(s_table, 1)

            def spread(l, c):
                act.wait_ge(s_centered[l], c + 1)
                nc.scalar.activation(sq[:, :, :], chunk(h, c), ACT.Square).then_inc(s_sq[l], 1)
                act.wait_ge(s_var[l], c + 1)
                nc.scalar.activation(std[:, :], var[:, :], ACT.Sqrt, bias=eps[:, :], scale=1.0 / D)\
                    .then_inc(s_std[l], 1)

            spread(0, 0)
            act.wait_ge(s_src, 48)
            nc.scalar.activation(nat[SRC], nat_i[SRC], ACT.Copy).then_inc(s_srcf, 1)
            spread(0, 1)
            act.wait_ge(s_cops, 1)
            nc.scalar.activation(coT[:, :], ps[0:NB, 4, 0:R[1]], ACT.Copy).then_inc(s_coT, 1)
            spread(0, 2)
            act.wait_ge(s_srcps, 1)
            nc.scalar.activation(srcT[:, :, :], ps_flat[:, 0:GT * P].rearrange("p (c g) -> p g c", c=GT)[:, 0:G, :],
                                 ACT.Copy).then_inc(s_srcT, 1)
            for c in range(3, NCH):
                spread(0, c)

            for l in range(2):
                if l == 1:
                    for b in range(2):
                        for u in range(UNITS):
                            act.wait_ge(s_gath[0][b][u], gathers(0, G - 2 + b, b, u))

                def senders(g, b, first=False):
                    if not first:
                        for u in range(UNITS):
                            act.wait_ge(s_gath[l][b][u], gathers(l, g - 2, b, u))
                    nc.scalar.activation(idx[:, b, :], srcT[:, bass.ds(g, 1), :].rearrange("p a c -> p (a c)"),
                                         ACT.Copy).then_inc(s_idx[l], 1)

                def aggregates(g):
                    wins, _ = group_counts(act, g)
                    with act.Fori(0, wins):
                        k = act_wins.value()
                        for u in range(UNITS):
                            if u == 0:
                                act.wait_ge(s_y[l], k + 1)
                            act.wait_ge(s_tiles[l], k * UNITS + (u + 1))
                            nc.scalar.activation(agg[0:MP[l], :, u * BANKT:(u + 1) * BANKT, :]
                                                 .rearrange("p r c n -> p c r n"),
                                                 ps[0:MP[l], u, :].rearrange("p (c r n) -> p c r n", c=BANKT, r=RC),
                                                 ACT.Copy).then_inc(s_agg[l], 1)
                        act_wins.add(1)

                act.sem_inc(s_offset[l], 1)
                act.wait_ge(s_srcT, 1)
                for b in range(2):
                    senders(b, b, first=True)

                def highest_part():
                    act.wait_ge(s_h[l], NCH)
                    nc.scalar.activation(h3[:, :, 0, :], h[:, :, :], ACT.Copy).then_inc(s_hi[l], 1)

                if l == 0:
                    highest_part()
                    act.wait_ge(s_w1ps, 1)
                    nc.scalar.activation(W[1][:, :, :], ps_flat[:, 2048:2048 + D * RC]
                                         .rearrange("i (o r) -> i r o", r=RC), ACT.Copy).then_inc(s_w1, 1)
                    for k, bank in enumerate((0, 4)):
                        act.wait_ge(s_keyps, k + 1)
                        nc.scalar.activation(keyT[k][:, 0:G, :], ps_flat[:, bank * 512:bank * 512 + GT * P]
                                             .rearrange("p (c g) -> p g c", c=GT)[:, 0:G, :], ACT.Copy)\
                            .then_inc(s_keyT, 1)
                    act.wait_ge(s_keyT, 2)
                    act.wait_ge(s_rows, 3)
                else:
                    def take_hT(c):
                        act.wait_ge(s_hTps, c + 1)
                        nc.scalar.activation(hT[:, c * CP:(c + 1) * CP, :],
                                             ps_hT[c % 2].rearrange("p (j n) -> p j n", j=CP), ACT.Copy)\
                            .then_inc(s_hT, 1)

                    for c in range(NCH):
                        spread(1, c)
                        if c >= 2:
                            take_hT(c - 2)
                    take_hT(NCH - 2)
                    take_hT(NCH - 1)
                    highest_part()

                for c in range(NCH):
                    act.wait_ge(s_rest[l], c + 1)
                    nc.scalar.activation(chunk(h3, c)[:, :, 1, :], chunk(rest, c), ACT.Copy).then_inc(s_mid[l], 1)
                act.sem_inc(s_agg[l], UNITS)
                act_wins.zero()
                with act.Fori(0, G // 2 - 1) as i:
                    for b in range(2):
                        pick = i * 2 + b
                        act.wait_ge(s_srcB[l], pick * 16 + 16)
                        act.wait_ge(s_sends[l], pick + 1)
                        nc.scalar.activation(offset[:, :], srcB[:, :], ACT.Identity, bias=first[:, :])\
                            .then_inc(s_offset[l], 1)
                        aggregates(i * 2 + b)
                        senders(i * 2 + (b + 2), b)
                for g in range(G - 2, G):
                    aggregates(g)

        @block.tensor
        def _(pe):
            pe_wins = Count(pe, "pe_wins", MAXW * G)
            pe_spans = Count(pe, "pe_spans", MAXW * MAXV * G)

            def turn_edges(a, bank, done):
                for c in range(GT):
                    last = nc.tensor.transpose(ps_flat[:, bank * 512 + c * P:bank * 512 + c * P + G],
                                               nat[a][:, c * P:(c + 1) * P], ident[0:G, 0:G])
                last.then_inc(done, 1)

            pe.wait_ge(s_ident, 1)
            pe.wait_ge(s_srcf, 1)
            turn_edges(SRC, 0, s_srcps)
            pe.wait_ge(s_basis, 32)
            nc.tensor.transpose(ps[0:NB, 4, 0:R[1]], co[:, :], ident[0:R[1], 0:R[1]]).then_inc(s_cops, 1)
            pe.wait_ge(s_coT, 1)
            bas_v = bas.rearrange("b (i o) -> b o i", o=D)
            for o in range(D):
                for half in range(2):
                    last = nc.tensor.matmul(ps_flat[half * D:(half + 1) * D, 2048 + o * RC:2048 + (o + 1) * RC],
                                            bas_v[:, o, :], coT[:, half * RC:(half + 1) * RC], start=True, stop=True)
            last.then_inc(s_w1ps, 1)
            pe.wait_ge(s_keys, 1)
            pe.wait_ge(s_srcT, 1)
            turn_edges(T16, 0, s_keyps)
            pe.wait_ge(s_gm, 1)
            nc.tensor.transpose(ps_rel, trel[0:G, :], ident[0:G, 0:G]).then_inc(s_tminps, 1)
            for j, a in enumerate((GMIN, GW, GV)):
                last = nc.tensor.matmul(ps_rows[:, j * P:j * P + G], gm[0:G, a:a + 1], ident[0:G, 0:G],
                                        start=True, stop=True)
            last.then_inc(s_rowps, 1)
            pe.wait_ge(s_tminT, 1)
            pe.wait_ge(s_rep, 2)
            nc.tensor.matmul(ps_slot, rep[:, :], tminT[:, 0:G], start=True, stop=True).then_inc(s_tminps, 1)
            pe.wait_ge(s_keys, 2)
            pe.wait_ge(s_w1, 1)
            pe.wait_ge(s_rows, 3)
            turn_edges(T32, 4, s_keyps)
            pe.wait_ge(s_keyT, 2)
            pe.wait_ge(s_w, 64)

            def turn_sums(l, c):
                if c == 0:
                    pe.wait_ge(s_acc[l], pe_spans.value() + 1)
                if c >= 2:
                    pe.wait_ge(s_outev[l], c - 1)
                for t in range(CH):
                    last = nc.tensor.transpose(ps_out[c % 2][:, t // 5, t % 5, 0:D1], accT_t[:, c * CH + t, :],
                                               ident[0:D1, 0:D1])
                last.then_inc(s_outps[l], 1)

            def turn_h(c):
                pe.wait_ge(s_h[1], c + 1)
                if c >= 2:
                    pe.wait_ge(s_hT, c - 1)
                for j in range(CP):
                    t = c * CH + 2 * j
                    last = nc.tensor.transpose(ps_hT[c % 2][:, j * P:(j + 1) * P],
                                               h[:, t:t + 2, :].rearrange("p t f -> p (t f)"), ident[:, :])
                last.then_inc(s_hTps, 1)

            for l in range(2):
                if l == 1:
                    for c in range(NCH):
                        turn_sums(0, c)
                        if c >= 2:
                            turn_h(c - 2)
                    turn_h(NCH - 2)
                    turn_h(NCH - 1)
                    pe.wait_ge(s_hT, NCH)
                    pe.wait_ge(s_outev[0], NCH)
                    for j in range(TT // 2):
                        last = nc.tensor.matmul(ps_self[:, j * P:(j + 1) * P], hT[:, j, :], selfW[:, :],
                                                start=True, stop=True)
                    last.then_inc(s_selfps, 1)
                    pe.wait_ge(s_self, 1)

                def pick_rows(pick):
                    pe.wait_ge(s_sends[l], pick + 2)
                    pe.wait_ge(s_picked[l], pick + 1)
                    for t in range(TT):
                        last = nc.tensor.matmul(ps_pick, sends[:, t, :], h3[:, t, :, :].rearrange("p a f -> p (a f)"),
                                                start=(t == 0), stop=(t == TT - 1))
                    last.then_inc(s_pickps[l], 1)

                def sum_group(g, b, pick=None):
                    wins, spans = group_counts(pe, g)
                    with pe.Fori(0, wins) as w:
                        k = pe_wins.value()
                        for c in range(GT):
                            u, i = divmod(c, BANKT)
                            if i == 0:
                                pe.wait_ge(s_gath[l][b][u], gathers(l, g, b, u))
                                if b == 0 and u == UNITS - 1:
                                    pe.wait_ge(s_picked[l], (g >> 1) * PICKS + 1)
                                pe.wait_ge(s_agg[l], k * UNITS + (u + 1))
                                pe.wait_ge(s_hot[l], k * UNITS + (u + 1))
                            for half in range(HALVES[l]):
                                last = nc.tensor.matmul(ps[half * D:half * D + M[l], u, i * COLS:(i + 1) * COLS],
                                                        gath[:, b, c, 0:M[l]],
                                                        hot_v[l][:, c, half * COLS:(half + 1) * COLS],
                                                        start=True, stop=True)
                            if i == BANKT - 1:
                                last.then_inc(s_tiles[l], 1)
                        pe.wait_ge(s_agg[l], k * UNITS + 2 * UNITS)
                        pe.wait_ge(s_y[l], k + 1)
                        for r in range(RC):
                            last = nc.tensor.matmul(ps_y[l], agg[0:MP[l], r, :, :].rearrange("i c n -> i (c n)"),
                                                    W[l][:, r, :], start=(r == 0), stop=(r == RC - 1))
                        last.then_inc(s_yps[l], 1)
                        with pe.If(w + 1 >= wins):
                            pe.sem_inc(s_group[l], 1)
                            if pick is not None:
                                pick_rows(pick)
                        with pe.Fori(0, spans):
                            a = pe_spans.value()
                            pe.wait_ge(s_y[l], k + 2)
                            pe.wait_ge(s_slothot[l], a + 1)
                            nc.tensor.matmul(ps_acc[l], y[:, 0:M[l]], slothot[:, :], start=True, stop=True)\
                                .then_inc(s_span[l], 1)
                            pe_spans.add(1)
                        pe_wins.add(1)

                pe_wins.zero()
                pe_spans.zero()
                with pe.Fori(0, G // 2 - 1) as i:
                    for b in range(2):
                        sum_group(i * 2 + b, b, pick=i * 2 + b)
                sum_group(G - 2, 0)
                sum_group(G - 1, 1)
            for c in range(NCH):
                turn_sums(1, c)

        @block.vector
        def _(dve):
            nc.vector.memset(eps[:, :], EPS).then_inc(s_eps, 1)
            nc.vector.memset(xs[96:P, 0:CH, :], 0.0).then_inc(s_xzero[0], 1)
            for a in (SRC, DST, T16, T32):
                nc.vector.memset(nat_i[a][96:G, LASTE:GE], NO_EDGE if a in (T16, T32) else 0).then_inc(s_pad, 1)
            dve.wait_ge(s_wzero, 1)
            nc.vector.memset(W[0][D:D1, :, D:D1], 1.0).then_inc(s_wzero, 1)
            for l in range(2):
                nc.vector.memset(keyT[l][:, G:G + 1, :], -1.0).then_inc(s_keypad, 1)

            dve_wins = Count(dve, "dve_wins", MAXW * G)
            dve_spans = Count(dve, "dve_spans", MAXW * MAXV * G)

            def wide(v):
                return v[:, :].rearrange("p (t a) -> p t a", a=1).broadcast_to([P, CH, D])

            def center(l, c):
                if l == 1:
                    x4 = chunk(xs, c).rearrange("p (b t) f -> p b t f", b=2)
                    dve.wait_ge(s_outps[0], c + 1)
                    nc.vector.tensor_tensor(x4, x4, ps_out[c % 2][:, :, :, 0:D], ALU.add).then_inc(s_xsum, 1)
                    nc.vector.tensor_scalar(rdeg[:, c * CH:(c + 1) * CH]
                                            .rearrange("p (b t a) -> p b t a", b=2, a=1),
                                            ps_out[c % 2][:, :, :, D:D1], 1.0, None, ALU.max).then_inc(s_outev[0], 1)
                    dve.wait_ge(s_xsum, c + 1)
                ln[l].step(nc.vector.tensor_reduce(out=sums[:, :], in_=chunk(xs, c), axis=AX.X, op=ALU.add))
                nc.vector.scalar_tensor_tensor(chunk(h, c), wide(sums), -1.0 / D, chunk(xs, c), ALU.mult, ALU.add)\
                    .then_inc(s_centered[l], 1)

            def variance(l, c):
                dve.wait_ge(s_sq[l], c + 1)
                nc.vector.tensor_reduce(out=var[:, :], in_=sq[:, :, :], axis=AX.X, op=ALU.add)\
                    .then_inc(s_var[l], 1)

            def scale(l, c):
                dve.wait_ge(s_std[l], c + 1)
                ln[l].step(nc.vector.reciprocal(rstd[:, :], std[:, :]))
                nc.vector.scalar_tensor_tensor(chunk(h, c), chunk(h, c), 0.0, wide(rstd), ALU.max, ALU.mult)\
                    .then_inc(s_h[l], 1)

            ln = [Chain(dve, s_ln[l]) for l in range(2)]

            def layernorm(l):
                for c in range(NCH):
                    if l == 0 and c < 2:
                        dve.wait_ge(s_xzero[c], 1)
                        dve.wait_ge(s_x[c], 48)
                    center(l, c)
                    if c > 0:
                        scale(l, c - 1)
                    variance(l, c)
                scale(l, NCH - 1)

            layernorm(0)

            def tiles(t):
                return t.rearrange("g (c p) -> g c p", p=P)

            setup = Chain(dve, s_setup)
            dve.wait_ge(s_edges, 16 * (9 + 1 + (REST > 0)))
            setup.step(nc.vector.tensor_reduce(out=tmin[0:G, :], in_=tiles(nat_i[DST]), axis=AX.X, op=ALU.min))
            setup.step(nc.vector.tensor_reduce(out=tmax[0:G, :], in_=tiles(nat_i[DST]), axis=AX.X, op=ALU.max))
            setup.step(nc.vector.tensor_tensor(tiles(nat[DST]), tiles(nat_i[DST]),
                                               tmin[0:G, :].rearrange("g (c a) -> g c a", a=1).broadcast_to([G, GT, P]),
                                               ALU.subtract))

            def keys(l, a):
                nc.vector.scalar_tensor_tensor(nat[a], nat[DST], float(R[l]), nat_i[a], ALU.mult, ALU.add)\
                    .then_inc(s_keys, 1)

            keys(0, T16)
            setup.step(nc.vector.tensor_reduce(out=gm[0:G, GMIN:GMIN + 1], in_=tmin[0:G, :], axis=AX.X, op=ALU.min))
            setup.step(nc.vector.tensor_reduce(out=gm[0:G, GMAX:GMAX + 1], in_=tmax[0:G, :], axis=AX.X, op=ALU.max))
            setup.step(nc.vector.tensor_tensor(tmax[0:G, :], tmax[0:G, :], tmin[0:G, :], ALU.subtract))
            setup.step(nc.vector.tensor_scalar(trel[0:G, :], tmin[0:G, :], gm[0:G, GMIN:GMIN + 1], None, ALU.subtract))
            setup.step(nc.vector.tensor_reduce(out=gi[0:G, 0:1], in_=tmax[0:G, :], axis=AX.X, op=ALU.max))
            setup.step(nc.vector.tensor_tensor(gi[0:G, 1:2], gm[0:G, GMAX:GMAX + 1], gm[0:G, GMIN:GMIN + 1],
                                               ALU.subtract))
            for j, n in enumerate((NW, SPAN)):
                setup.step(nc.vector.tensor_scalar(gj[0:G, j:j + 1], gi[0:G, j:j + 1], n.bit_length() - 1, None,
                                                   ALU.arith_shift_right))
            nc.vector.tensor_scalar(gm[0:G, GW:GV + 1], gj[0:G, :], 1.0, None, ALU.add).then_inc(s_gm, 1)
            keys(1, T32)
            dve.wait_ge(s_lane, 1)
            setup.step(nc.vector.tensor_scalar(lane8i[:, :], lane[:, :], NW - 1, None, ALU.bitwise_and))
            setup.step(nc.vector.tensor_copy(lane8[:, :], lane8i[:, :]))
            dve.wait_ge(s_tminps, 1)
            nc.vector.tensor_copy(tminT[:, 0:G], ps_rel).then_inc(s_tminT, 1)
            dve.wait_ge(s_rowps, 1)
            nc.vector.tensor_copy(rowf[:, :, 0:G], ps_rows.rearrange("p (a g) -> p a g", a=3)[:, :, 0:G])\
                .then_inc(s_rowf, 1)
            dve.wait_ge(s_rowf, 1)
            nc.vector.tensor_copy(rows[:, BASE, 0:G], rowf[:, BASE, 0:G]).then_inc(s_rows, 1)
            nc.vector.scalar_tensor_tensor(rows[:, COUNTS, 0:G], rowf[:, WINS, 0:G], float(1 << VBITS),
                                           rowf[:, SPANS, 0:G], ALU.mult, ALU.add).then_inc(s_rows, 1)
            dve.wait_ge(s_tminps, 2)
            nc.vector.tensor_scalar(slot[:, :], ps_slot, lane8[:, :], None, ALU.add).then_inc(s_rows, 1)

            for l in range(2):
                if l == 1:
                    dve.wait_ge(s_store[0], 16 * NCH)
                    layernorm(1)
                nc.vector.memset(slotw[:, :], 0.0).then_inc(s_slotw[l], 1)
                nc.vector.memset(slotv[:, :], 0.0).then_inc(s_spanstep[l], 1)
                nc.vector.memset(y[:, :], 0.0).then_inc(s_y[l], 1)
                dve.wait_ge(s_const, 6)
                dve.wait_ge(s_rows, 3)
                dve.wait_ge(s_keyT, 1 + l)
                dve.wait_ge(s_keypad, 2)
                dve.wait_ge(s_srcT, 1)
                dve_wins.zero()
                dve_spans.zero()

                def build_onehot(u):
                    nc.vector.tensor_tensor(
                        hot_v[l][:, u * BANKT:(u + 1) * BANKT, :],
                        iotaK[l][:, :, :, :].rearrange("p (a h) r n -> p a (h r n)", a=1)
                        .broadcast_to([P, BANKT, KEYS[l]]),
                        keyw[:, u * BANKT:(u + 1) * BANKT].rearrange("p (c a) -> p c a", a=1)
                        .broadcast_to([P, BANKT, KEYS[l]]), ALU.is_equal).then_inc(s_hot[l], 1)

                nc.vector.tensor_copy(keyw[:, :], keyT[l][:, 0, :]).then_inc(s_keyw[l], 1)
                dve.wait_ge(s_keyw[l], 1)
                for u in range(UNITS):
                    build_onehot(u)

                if l == 1:
                    dve.wait_ge(s_selfps, 1)
                    xf = xs[:, :, :].rearrange("p t f -> p (t f)")
                    nc.vector.tensor_tensor(xf, xf, ps_self, ALU.add).then_inc(s_self, 1)
                dve.wait_ge(s_w1, 1)
                dve.wait_ge(s_hi[l], 1)
                for c in range(NCH):
                    nc.vector.tensor_tensor(chunk(rest, c), chunk(h, c), chunk(h3, c)[:, :, 0, :], ALU.subtract)\
                        .then_inc(s_rest[l], 1)
                for c in range(NCH):
                    dve.wait_ge(s_mid[l], c + 1)
                    nc.vector.tensor_tensor(chunk(h3, c)[:, :, 2, :], chunk(rest, c), chunk(h3, c)[:, :, 1, :],
                                            ALU.subtract).then_inc(s_lo[l], 1)
                dve.wait_ge(s_lo[l], NCH)
                dve.sem_inc(s_sends[l], 1)
                dve.sem_inc(s_picked[l], 1)

                def build_sends(pick):
                    dve.wait_ge(s_offset[l], pick + 2)
                    nc.vector.tensor_tensor(sends.rearrange("p t (k e) -> p t k e", e=8),
                                            offset[:, :].rearrange("p (a k e) -> p a k e", a=1, e=8)
                                            .broadcast_to([P, TT, P // 8, 8]),
                                            iotaT[:, :, :].rearrange("p t (a e) -> p t a e", a=1)
                                            .broadcast_to([P, TT, P // 8, 8]), ALU.is_equal).then_inc(s_sends[l], 1)

                def take_picked(pick, b):
                    dve.wait_ge(s_pickps[l], pick + 1)
                    nc.vector.tensor_reduce(out=gath[:, 0, GT - PICKS + b, 0:D],
                                            in_=ps_pick.rearrange("p (a f) -> p f a", a=3), axis=AX.X, op=ALU.add)\
                        .then_inc(s_picked[l], 1)

                dve.wait_ge(s_zeroed[l], (1, NCH)[l])
                dve.sem_inc(s_acc[l], 1)

                def add_group(g):
                    wins, spans = group_counts(dve, g)
                    base = dve.value_load(rows[0:1, BASE, bass.ds(g, 1)], min_val=0, max_val=N - 1)
                    dve.wait_ge(s_slotw[l], dve_wins.value() + g + 1)
                    nc.vector.tensor_copy(slotw[:, :], slot[:, bass.ds(g, 1)]).then_inc(s_slotw[l], 1)
                    with dve.Fori(0, wins) as w:
                        k = dve_wins.value()
                        dve.wait_ge(s_slotw[l], k + g + 2)
                        dve.wait_ge(s_spanstep[l], dve_spans.value() + 1)
                        nc.vector.tensor_copy(slotv[:, :], slotw[:, :]).then_inc(s_slotv[l], 1)
                        dve.wait_ge(s_slotv[l], k + 1)
                        nc.vector.tensor_scalar(slotw[:, :], slotw[:, :], float(NW), None, ALU.add)\
                            .then_inc(s_slotw[l], 1)
                        dve.wait_ge(s_hot[l], k * UNITS + UNITS)
                        with dve.If(w + 1 < wins):
                            nc.vector.tensor_scalar(keyw[:, :], keyw[:, :], float(-KEYS[l]), None, ALU.add)\
                                .then_inc(s_keyw[l], 1)
                        with dve.Else():
                            nc.vector.tensor_copy(keyw[:, :], keyT[l][:, bass.ds(g + 1, 1), :]
                                                  .rearrange("p a c -> p (a c)")).then_inc(s_keyw[l], 1)
                        dve.wait_ge(s_keyw[l], k + 2)
                        for u in range(UNITS):
                            dve.wait_ge(s_tiles[l], k * UNITS + (u + 1))
                            build_onehot(u)
                        dve.wait_ge(s_yps[l], k + 1)
                        nc.vector.tensor_copy(y[:, 0:M[l]], ps_y[l]).then_inc(s_y[l], 1)
                        with dve.Fori(0, spans) as v:
                            a = dve_spans.value()
                            dve.wait_ge(s_spanstep[l], a + 1)
                            nc.vector.tensor_scalar(slothot[:, :], iotaS[:, :], slotv[:, :], None, ALU.is_equal)\
                                .then_inc(s_slothot[l], 1)
                            dve.wait_ge(s_slothot[l], a + 1)
                            nc.vector.tensor_scalar(slotv[:, :], slotv[:, :], float(-SPAN), None, ALU.add)\
                                .then_inc(s_spanstep[l], 1)
                            dve.wait_ge(s_span[l], a + 1)
                            dve.wait_ge(s_acc[l], a + 1)
                            start = nc.s_assert_within(
                                base + v * SPAN, 0, N - 1,
                                skip_runtime_bounds_check_because="it is at most the group's largest receiver")
                            win = accT[0:M[l], bass.ds(start, SPAN)]
                            nc.vector.tensor_tensor(win, win, ps_acc[l], ALU.add).then_inc(s_acc[l], 1)
                            dve_spans.add(1)
                        dve_wins.add(1)

                with dve.Fori(0, G // 2 - 1) as i:
                    for b in range(2):
                        build_sends(i * 2 + b)
                        add_group(i * 2 + b)
                        take_picked(i * 2 + b, b)
                if l == 1:
                    nc.vector.reciprocal(rdeg[:, :], rdeg[:, :]).then_inc(s_base, 1)
                    dve.wait_ge(s_self, 1)
                    dve.wait_ge(s_w, 64)
                    nc.vector.tensor_tensor(xs[:, :, :], xs[:, :, :], biasB[:, :, :].broadcast_to([P, TT, D]), ALU.add)\
                        .then_inc(s_base, 1)
                for g in range(G - 2, G):
                    add_group(g)

            dve.wait_ge(s_base, 2)
            dve.wait_ge(s_store[1], 16 * NCH)
            for c in range(NCH):
                dve.wait_ge(s_outps[1], c + 1)
                nc.vector.tensor_tensor(chunk(h, c).rearrange("p (b t) f -> p b t f", b=2),
                                        ps_out[c % 2][:, :, :, 0:D],
                                        rdeg[:, c * CH:(c + 1) * CH].rearrange("p (b t a) -> p b t a", b=2, a=1)
                                        .broadcast_to([P, 2, 5, D]), ALU.mult).then_inc(s_outev[1], 1)
                dve.wait_ge(s_outev[1], c + 1)
                nc.vector.tensor_tensor(chunk(h, c), chunk(h, c), chunk(xs, c), ALU.add).then_inc(s_final, 1)


_INS = ["x", "src", "dst", "edge_type_16", "edge_type_32", "L0_gnn_weight", "L1_gnn_basis", "L1_gnn_coeff",
        "L1_gnn_self_weight", "L1_gnn_bias"]


def kernel(**inputs):
    import numpy as np
    import concourse.bacc as bacc
    from concourse import mybir as mb
    from concourse.bass_utils import run_bass_kernel_spmd

    nc = bacc.Bacc("TRN2", target_bir_lowering=False, num_devices=1)
    arrays, args = {}, []
    for name in _INS:
        a = np.ascontiguousarray(inputs[name])
        arrays[f"in_{name}"] = a
        args.append(nc.dram_tensor(f"in_{name}", a.shape, mb.dt.from_np(a.dtype), kind="ExternalInput").ap())
    shape = arrays["in_x"].shape
    args.append(nc.dram_tensor("out_x", shape, mb.dt.float32, kind="ExternalOutput").ap())
    two_layer_gnn_kernel(nc, *args)
    r = run_bass_kernel_spmd(nc, [arrays], core_ids=[0])
    return r.results[0]["out_x"]
```
